# Optimizing a Trainium2 kernel written in Bass

```python
import numpy as np
import jax
import jax.numpy as jnp

def _softmax(x, axis=-1):
    return jax.nn.softmax(x, axis=axis)

def _gelu(x):
    return jax.nn.gelu(x, approximate=True)

def _silu(x):
    return jax.nn.silu(x)

def _sigmoid(x):
    return jax.nn.sigmoid(x)

def _layernorm(x, axis=-1, eps=1e-05):
    m = jnp.mean(x, axis=axis, keepdims=True)
    v = jnp.var(x, axis=axis, keepdims=True)
    return (x - m) / jnp.sqrt(v + eps)

def _scatter_add(tgt, idx, src, axis=0):
    return tgt.at[idx].add(src)

def _segment_sum(src, seg, n):
    return jax.ops.segment_sum(src, seg, n)
kernel_name = 'mk_prb_d1_jaxref_r8_edb984'

def setup_inputs(seed: int=0):
    np.random.seed(seed)
    _w = jnp.asarray

    def _L0_attn_setup():
        import jax, jax.numpy as jnp
        import numpy as np
        DIM = 128
        NUM_HEADS = 16
        HEAD_DIM = DIM // NUM_HEADS
        NB_FEATURES = 32

        def _kernel_feature_map(x, proj):
            z = jnp.einsum('bhtd,hdf->bhtf', x, proj)
            return jnp.exp(z - jnp.max(z, axis=-1, keepdims=True))
        key = jax.random.key(seed)
        k1, k2, k3, k4, k5 = jax.random.split(key, 5)
        x = jax.random.normal(k1, (4, 512, DIM), dtype=jnp.float32)
        w_qkv = jax.random.normal(k2, (DIM, 3 * DIM), dtype=jnp.float32) / np.sqrt(DIM)
        w_out = jax.random.normal(k3, (DIM, DIM), dtype=jnp.float32) / np.sqrt(DIM)
        b_out = jnp.zeros((DIM,), dtype=jnp.float32)
        proj = 0.05 * jax.random.normal(k4, (NUM_HEADS, HEAD_DIM, NB_FEATURES), dtype=jnp.float32)
        return {'x': x, 'w_qkv': w_qkv, 'w_out': w_out, 'b_out': b_out, 'proj': proj}
    _L0_attn_in = _L0_attn_setup()

    def _L0_ffn_setup():
        import jax, jax.numpy as jnp
        import numpy as np
        B, T, D, E, FF, K = (4, 128, 128, 8, 256, 2)
        SINKHORN_ITERS = 3

        def _sinkhorn(log_alpha, iters=SINKHORN_ITERS):
            for _ in range(iters):
                log_alpha = log_alpha - jax.nn.logsumexp(log_alpha, axis=-1, keepdims=True)
                log_alpha = log_alpha - jax.nn.logsumexp(log_alpha, axis=-2, keepdims=True)
            gates = jnp.exp(log_alpha)
            return gates / (jnp.sum(gates, axis=-1, keepdims=True) + 1e-08)
        key = jax.random.key(seed)
        ks = jax.random.split(key, 7)
        scale = 0.02
        return {'x': jax.random.normal(ks[0], (B, T, D), dtype=jnp.float32), 'router_w': jax.random.normal(ks[1], (E, D), dtype=jnp.float32) * scale, 'router_b': jnp.zeros((E,), dtype=jnp.float32), 'temperature': jnp.ones((1,), dtype=jnp.float32) * 0.5, 'wg': jax.random.normal(ks[2], (E, D, FF), dtype=jnp.float32) * scale, 'wp': jax.random.normal(ks[3], (E, D, FF), dtype=jnp.float32) * scale, 'wo': jax.random.normal(ks[4], (E, FF, D), dtype=jnp.float32) * scale}
    _L0_ffn_in = _L0_ffn_setup()
    _d = {'L0_attn_x': _L0_attn_in['x'], 'L0_attn_w_qkv': _L0_attn_in['w_qkv'], 'L0_attn_w_out': _L0_attn_in['w_out'], 'L0_attn_b_out': _L0_attn_in['b_out'], 'L0_attn_proj': _L0_attn_in['proj'], 'L0_ffn_router_w': _L0_ffn_in['router_w'], 'L0_ffn_router_b': _L0_ffn_in['router_b'], 'L0_ffn_temperature': _L0_ffn_in['temperature'], 'L0_ffn_wg': _L0_ffn_in['wg'], 'L0_ffn_wp': _L0_ffn_in['wp'], 'L0_ffn_wo': _L0_ffn_in['wo']}
    _x0 = _d['L0_attn_x']
    _d['L0_attn_x'] = jax.random.normal(jax.random.fold_in(jax.random.key(seed), 1), (16, 256, 128), dtype=_x0.dtype)
    del _x0
    return _d

def reference(L0_attn_x, L0_attn_w_qkv, L0_attn_w_out, L0_attn_b_out, L0_attn_proj, L0_ffn_router_w, L0_ffn_router_b, L0_ffn_temperature, L0_ffn_wg, L0_ffn_wp, L0_ffn_wo):

    def _L0_attn_ref(x, w_qkv, w_out, b_out, proj):
        import jax, jax.numpy as jnp
        import numpy as np
        DIM = 128
        NUM_HEADS = 16
        HEAD_DIM = DIM // NUM_HEADS
        NB_FEATURES = 32

        def _kernel_feature_map(x, proj):
            z = jnp.einsum('bhtd,hdf->bhtf', x, proj)
            return jnp.exp(z - jnp.max(z, axis=-1, keepdims=True))
        B, T, _ = x.shape
        qkv = x @ w_qkv
        q, k, v = jnp.split(qkv, 3, axis=-1)

        def to_heads(t):
            return t.reshape(B, T, NUM_HEADS, HEAD_DIM).transpose(0, 2, 1, 3)
        q, k, v = (to_heads(q), to_heads(k), to_heads(v))
        q_prime = _kernel_feature_map(q, proj)
        k_prime = _kernel_feature_map(k, proj)
        kv = jnp.einsum('bhtf,bhtd->bhfd', k_prime, v)
        k_sum = jnp.sum(k_prime, axis=2)
        z = 1.0 / (jnp.einsum('bhtf,bhf->bht', q_prime, k_sum) + 1e-06)
        out = jnp.einsum('bhtf,bhfd,bht->bhtd', q_prime, kv, z)
        out = out.transpose(0, 2, 1, 3).reshape(B, T, DIM)
        return out @ w_out + b_out

    def _L0_ffn_ref(x, router_w, router_b, temperature, wg, wp, wo):
        import jax, jax.numpy as jnp
        import numpy as np
        B, T, D, E, FF, K = (4, 128, 128, 8, 256, 2)
        SINKHORN_ITERS = 3

        def _sinkhorn(log_alpha, iters=SINKHORN_ITERS):
            for _ in range(iters):
                log_alpha = log_alpha - jax.nn.logsumexp(log_alpha, axis=-1, keepdims=True)
                log_alpha = log_alpha - jax.nn.logsumexp(log_alpha, axis=-2, keepdims=True)
            gates = jnp.exp(log_alpha)
            return gates / (jnp.sum(gates, axis=-1, keepdims=True) + 1e-08)
        temp = jnp.maximum(temperature, 0.1)
        scores = (jnp.einsum('btd,ed->bte', x, router_w) + router_b) / temp
        gates = _sinkhorn(scores)
        topk_vals, topk_idx = jax.lax.top_k(gates, K)
        topk_gates = topk_vals / (jnp.sum(topk_vals, axis=-1, keepdims=True) + 1e-08)
        g = jax.nn.relu(jnp.einsum('btd,edf->btef', x, wg))
        p = jnp.einsum('btd,edf->btef', x, wp)
        all_out = jnp.einsum('btef,efd->bted', g * p, wo)
        gathered = jnp.take_along_axis(all_out, topk_idx[..., None], axis=2)
        expert_out = jnp.sum(gathered * topk_gates[..., None], axis=2)
        return x + expert_out
    x = L0_attn_x
    xn = _layernorm(x, axis=-1)
    x = x + _L0_attn_ref(xn, L0_attn_w_qkv, L0_attn_w_out, L0_attn_b_out, L0_attn_proj) + _L0_ffn_ref(xn, L0_ffn_router_w, L0_ffn_router_b, L0_ffn_temperature, L0_ffn_wg, L0_ffn_wp, L0_ffn_wo)
    return x

_drawn_inputs = setup_inputs


def setup_inputs(seed=0):
    import zlib

    import numpy as np

    out = dict(_drawn_inputs(seed))
    spreads = {'L0_attn_b_out': (0.0, 0.465), 'L0_ffn_router_b': (0.0, 0.8)}
    factors = {'L0_attn_proj': 64.0,
     'L0_ffn_router_w': 8.0,
     'L0_ffn_wg': 8.0,
     'L0_ffn_wp': 8.0,
     'L0_ffn_wo': 8.0,
     'L0_attn_w_qkv': 4.113,
     'L0_attn_w_out': 4.08}
    for name, (base, spread) in spreads.items():
        noise = np.random.default_rng([zlib.crc32(name.encode()), seed]).standard_normal(out[name].shape)
        drawn = base * np.exp(spread * noise) if base else spread * noise
        out[name] = jnp.asarray(drawn.astype(out[name].dtype))
    for name, factor in factors.items():
        out[name] = (out[name] * factor).astype(out[name].dtype)
    return out
```

```python
from contextlib import ExitStack

import concourse.bass as bass
from concourse import mybir

F32 = mybir.dt.float32
I32 = mybir.dt.int32
ALU = mybir.AluOpType
ACT = mybir.ActivationFunctionType
AX_X = mybir.AxisListType.X

P = 128
LN_EPS = 1e-5
DEN_EPS = 1e-6
GATE_EPS = 1e-8
SINKHORN_ITERS = 3
EXP_LN_TABLE = "natural_log_exp_and_others"


def build_program(nc, x, wqT, wkT, wv, w_out, b_out, proj, router_wT, router_b, temperature, w_expert, out):
    D = wv.shape[0]
    NT = x.shape[1] // D
    NB = NT // 2
    HEADS, F = 16, proj.shape[1]
    HD = D // HEADS
    E = router_wT.shape[1]
    FF = w_expert.shape[2] // 3
    FC = FF // P
    FEAT = HEADS * F
    CH = FEAT // P
    HC = HEADS // CH
    VC = HC * HD
    AUG = VC + HC
    TOPK = 2
    ST = 256
    SLOT_TILES = (NT * P * TOPK - E) // ST + E
    GROUP = 4
    NG = NT // GROUP
    RING = 8
    ROUTED = 4
    EARLY = 10

    slots_x = nc.dram_tensor("slots_x", [SLOT_TILES * ST, D], F32, kind="Internal").ap()
    slots_y = nc.dram_tensor("slots_y", [SLOT_TILES * ST, D], F32, kind="Internal").ap()

    with ExitStack() as ctx:
        def sb(name, shape, dt=F32):
            return ctx.enter_context(nc.sbuf_tensor(name, shape, dt))

        def sem(name):
            return ctx.enter_context(nc.semaphore(name))

        ident = sb("ident", [P, P])
        ones = sb("ones", [P, P])
        earlier = sb("earlier", [P, P])
        head_of_row = sb("head_of_row", [P, HEADS])
        chunk_mask = sb("chunk_mask", [P, AUG])
        rank_of_expert = sb("rank_of_expert", [P, E])
        tile_number = sb("tile_number", [P, SLOT_TILES, E])
        scan_keep = sb("scan_keep", [P, E, NT])
        eps_tile = sb("eps_tile", [P, 1])
        zeros = sb("zeros", [P, 2 * D])

        acc = sb("acc", [P, NT, D])
        xn = sb("xn", [P, NT, D])
        xnT = sb("xnT", [P, NT * P])
        wqT_sb, wkT_sb, wv_sb, w_out_sb = (sb(n, [P, D]) for n in ("wqT_sb", "wkT_sb", "wv_sb", "w_out_sb"))
        b_out_sb = sb("b_out_sb", [P, D])
        proj_sb = sb("proj_sb", [P, F])
        proj_diag = sb("proj_diag", [P, HEADS, F])
        w_feat = sb("w_feat", [P, 2, FEAT])
        router_sb = sb("router_sb", [P, E])
        router_b_sb = sb("router_b_sb", [P, E])
        temp_sb = sb("temp_sb", [P, 1])
        temp_lim = sb("temp_lim", [P, 1])
        inv_temp = sb("inv_temp", [P, 1])
        stats = sb("stats", [P, NT, 6])
        moments = sb("moments", [P, NT, 2])
        std = sb("std", [P, NT])
        rstd = sb("rstd", [P, NT])

        xT_stage = [sb(f"xT_stage{i}", [P, 2 * P]) for i in range(2)]
        v_aug = [sb(f"v_aug{i}", [P, 2, CH, AUG]) for i in range(2)]
        neg_max = [sb(f"neg_max{n}", [P, HEADS]) for n in range(4)]
        z_sb = [sb(f"z_sb{n}", [P, FEAT]) for n in range(4)]
        feat = [[sb(f"feat{i}_{n}", [P, FEAT]) for n in range(4)] for i in range(2)]
        kv_sb = [sb(f"kv_sb{i}", [P, CH, AUG]) for i in range(2)]
        qT_sb = [sb(f"qT_sb{h}", [P, CH * P]) for h in range(2)]
        den = sb("den", [P, 2 * CH, HC])
        inv_den = sb("inv_den", [P, 2 * CH, HC])
        att = sb("att", [P, 2 * P])
        attT = sb("attT", [P, 2 * P])

        W = NT * E
        scores = sb("scores", [P, W])
        row_max, row_sum, row_ln = (sb(n, [P, NT]) for n in ("row_max", "row_sum", "row_ln"))
        row_shift, row_exp, row_log = (sb(n, [P, W]) for n in ("row_shift", "row_exp", "row_log"))
        col_negmax, col_sum, col_ln = (sb(n, [P, 1]) for n in ("col_negmax", "col_sum", "col_ln"))
        col_exp, col_log = (sb(n, [P, 2 * P]) for n in ("col_exp", "col_log"))
        gate_exp, gates, rest = (sb(n, [P, W]) for n in ("gate_exp", "gates", "rest"))
        gate_sum, gate_inv, best_rank = (sb(n, [P, NT]) for n in ("gate_sum", "gate_inv", "best_rank"))
        top = [sb(f"top{k}", [P, NT]) for k in range(TOPK)]
        chosen = [sb(f"chosen{k}", [P, W]) for k in range(TOPK)]
        is_best, ranked, mask = (sb(n, [P, W]) for n in ("is_best", "ranked", "mask"))
        top_sum, top_inv = sb("top_sum", [P, NT]), sb("top_inv", [P, NT])
        weight = [sb(f"weight{k}", [P, NT]) for k in range(TOPK)]
        totals, prefix, start = (sb(n, [P, E, NT]) for n in ("totals", "prefix", "start"))
        position, picked = sb("position", [P, W]), [sb(f"picked{k}", [P, W]) for k in range(TOPK)]
        padded_i, tiles_i = sb("padded_i", [P, E], I32), sb("tiles_i", [P, E], I32)
        tiles_f, tiles_end, first_slot = (sb(n, [P, E]) for n in ("tiles_f", "tiles_end", "first_slot"))
        slot_f = [sb(f"slot_f{k}", [P, NT]) for k in range(TOPK)]
        slot_i = [sb(f"slot_i{k}", [P, NT], I32) for k in range(TOPK)]
        past = sb("past", [P, SLOT_TILES, E])
        expert_f = sb("expert_f", [P, SLOT_TILES])
        expert_i = sb("expert_i", [P, SLOT_TILES], I32)

        w_up = [sb(f"w_up{i}", [P, 2 * FF]) for i in range(2)]
        w_down = [sb(f"w_down{i}", [P, FF]) for i in range(2)]
        x_tile = [sb(f"x_tile{i}", [P, 2, D]) for i in range(2)]
        xT_tile = [sb(f"xT_tile{i}", [P, ST]) for i in range(2)]
        gate_act = [sb(f"gate_act{i}", [P, FC * ST]) for i in range(2)]
        hidden = [sb(f"hidden{i}", [P, FC, ST]) for i in range(2)]
        y_tile = [sb(f"y_tile{i}", [P, 2, D]) for i in range(2)]
        y_back = sb("y_back", [P, RING, TOPK, D])

        bank = [ctx.enter_context(nc.psum_tensor(f"bank{i}", [P, 512], F32)) for i in range(8)]
        V_BANK, Z_BANK, QT_BANK, KV_BANK, ROUTE_BANK = 0, 1, 5, 6, 7
        ND = CH * AUG

        x_landed = [sem(f"x_landed{g}") for g in range(NG)]
        weights_landed, zeros_landed = sem("weights_landed"), sem("zeros_landed")
        zeros_set, consts_set, ident_set, chunk_mask_set = (
            sem(n) for n in ("zeros_set", "consts_set", "ident_set", "chunk_mask_set"))
        stats_done, moments_done, std_done, rstd_done, xn_ready = (
            sem(n) for n in ("stats_done", "moments_done", "std_done", "rstd_done", "xn_ready"))
        xnT_ready, xnT_copied, scores_ready, base_added = (
            sem(n) for n in ("xnT_ready", "xnT_copied", "scores_ready", "base_added"))
        diag_ready, w_feat_ready, w_feat_copied = sem("diag_ready"), sem("w_feat_ready"), sem("w_feat_copied")
        xT_staged = [sem(f"xT_staged{i}") for i in range(2)]
        z_ready, z_negmax, z_shifted, feat_ready = (
            sem(n) for n in ("z_ready", "z_negmax", "z_shifted", "feat_ready"))
        v_ready, v_copied, kv_ready, kv_masked = (sem(n) for n in ("v_ready", "v_copied", "kv_ready", "kv_masked"))
        qT_ready, qT_copied, nd_ready, den_step, att_ready = (
            sem(n) for n in ("qT_ready", "qT_copied", "nd_ready", "den_step", "att_ready"))
        attT_ready, attT_copied, proj_ready, acc_added = (
            sem(n) for n in ("attT_ready", "attT_copied", "proj_ready", "acc_added"))
        route_step = sem("route_step")
        row_shifted, row_exped, row_summed, row_lned, row_normed = (
            sem(n) for n in ("row_shifted", "row_exped", "row_summed", "row_lned", "row_normed"))
        cols_in, col_maxed, col_summed, col_lned, col_normed, rows_in = (
            sem(n) for n in ("cols_in", "col_maxed", "col_summed", "col_lned", "col_normed", "rows_in"))
        gates_exped, mask_ready, counts_ready, slots_ready, experts_ready = (
            sem(n) for n in ("gates_exped", "mask_ready", "counts_ready", "slots_ready", "experts_ready"))
        scattered = sem("scattered")
        w_up_landed = [sem(f"w_up_landed{i}") for i in range(2)]
        w_down_landed = [sem(f"w_down_landed{i}") for i in range(2)]
        rows_landed = [sem(f"rows_landed{i}") for i in range(2)]
        y_stored = [sem(f"y_stored{i}") for i in range(2)]
        xT_ready, xT_copied, up_ready, relu_done, hidden_ready, y_ready, y_copied = (
            sem(n) for n in ("xT_ready", "xT_copied", "up_ready", "relu_done", "hidden_ready", "y_ready", "y_copied"))
        gathered = [sem(f"gathered{i}") for i in range(RING)]
        first_added, combined, out_stored = sem("first_added"), sem("combined"), sem("out_stored")

        N_WEIGHTS = 9

        def routing_tile(j):
            return (j % 2) * NB + j // 2

        def by_tile(t):
            return t[:, :].rearrange("p (i e) -> p i e", e=E)

        def wide(t, n):
            return t[:, :].unsqueeze(2).broadcast_to([P, t.shape[1], n])

        def over_tiles(t, n):
            return t[:, :].unsqueeze(1).broadcast_to([P, n, t.shape[1]])

        def late(v, n):
            return not isinstance(v, int) or v >= n

        def attend_early(engine, step):
            step(-1, -1, 1, back=False, tail=False, route=True)
            step(0, 0, 0, tail=False, route=True)
            for b in range(1, ROUTED):
                step(b, b // 2, b % 2, route=True)
            with engine.Fori(ROUTED // 2, EARLY // 2 - 1) as i:
                step(2 * i, i, 0)
                step(2 * i + 1, i, 1)
            step(EARLY - 2, EARLY // 2 - 1, 0)
            step(EARLY - 1, EARLY // 2 - 1, 1, front=False)
            step(EARLY, EARLY // 2, 0, front=False, back=False)

        def attend_late(step):
            for b in range(EARLY - 1, NB + 1):
                step(b, b // 2, b % 2, front=b + 1 < NB, back=EARLY <= b < NB, tail=b > EARLY)

        def experts(engine, step):
            step(0, 0, 0)
            step(1, 0, 1)
            with engine.Fori(1, SLOT_TILES // 2 - 2) as i:
                step(2 * i, i, 0)
                step(2 * i + 1, i, 1)
            for k in range(SLOT_TILES // 2 * 2 - 4, SLOT_TILES):
                step(k, k // 2, k % 2)

        block = ctx.enter_context(nc.Block())

        @block.sync
        def _(sp):
            for g in range(NG):
                cols = slice(g * GROUP * D, (g + 1) * GROUP * D)
                sp.dma_start(acc[:, g * GROUP:(g + 1) * GROUP, :].rearrange("p j d -> p (j d)"),
                             x[:, cols]).then_inc(x_landed[g], 16)
            sp.wait_ge(zeros_set, 1)
            ZR = ST * SLOT_TILES // P
            for r in range(0, ZR, 2):
                rows = slots_x.rearrange("(p r) d -> p (r d)", p=P)
                sp.dma_start(rows[:, r * D:(r + 2) * D], zeros[:, :]).then_inc(zeros_landed, 16)

            def stage(f_half, par):
                f = 2 * f_half + par
                sp.wait_ge(z_ready, 4 * (f - 1))
                sp.wait_ge(v_ready, f - 1)
                src = xnT[:, bass.ds(f * (2 * P), 2 * P)]
                sp.dma_start(xT_stage[par][:, :], src).then_inc(xT_staged[par], 16)

            sp.wait_ge(xnT_copied, NG)
            with sp.Fori(ROUTED // 2, EARLY // 2 - 1) as i:
                stage(i, 1)
                stage(i + 1, 0)

            expert_reg = sp.alloc_register("expert_reg")
            ys = slots_y.rearrange("(k t p) d -> k p t d", t=2, p=P)
            xs = slots_x.rearrange("(k t p) d -> k p t d", t=2, p=P)

            def load_rows(k, par):
                if late(k, 2):
                    sp.wait_ge(xT_ready, k - 1)
                sp.dma_start(x_tile[par][:, :, :],
                             xs[bass.ds(k, 1), :, :, :].rearrange("a p t d -> (a p) t d"))\
                    .then_inc(rows_landed[par], 16)

            def expert_of(k):
                sp.reg_load(expert_reg, expert_i[0:1, bass.ds(k, 1)])
                return bass.ds(sp.snap(expert_reg, min_val=0, max_val=E - 1), 1)

            def load_up(k, par):
                e = expert_of(k)
                if late(k, 2):
                    sp.wait_ge(up_ready, 2 * k - 2)
                sp.dma_start(w_up[par][:, :], w_expert[e, :, 0:2 * FF].rearrange("a p n -> (a p) n"))\
                    .then_inc(w_up_landed[par], 16)

            def load_down(k, par):
                e = expert_of(k)
                if late(k, 2):
                    sp.wait_ge(y_ready, k - 1)
                sp.dma_start(w_down[par][:, :], w_expert[e, :, 2 * FF:3 * FF].rearrange("a p n -> (a p) n"))\
                    .then_inc(w_down_landed[par], 16)

            def store_tile(k, par):
                sp.wait_ge(y_copied, k + 1)
                sp.dma_start(ys[bass.ds(k, 1), :, :, :].rearrange("a p t d -> (a p) t d"),
                             y_tile[par][:, :, :]).then_inc(y_stored[par], 16)

            def expert_step(k, k_half, par):
                if not isinstance(k, int) or k + 4 < SLOT_TILES:
                    load_rows(k + 4, par)
                if not isinstance(k, int) or k + 3 < SLOT_TILES:
                    load_up(k + 3, 1 - par)
                if not isinstance(k, int) or k + 2 < SLOT_TILES:
                    load_down(k + 2, par)
                store_tile(k, par)

            sp.wait_ge(experts_ready, 1)
            load_up(0, 0)
            load_up(1, 1)
            load_down(0, 0)
            load_down(1, 1)
            sp.wait_ge(scattered, 16 * NT * TOPK)
            for k in range(4):
                load_rows(k, k % 2)
            load_up(2, 0)
            experts(sp, expert_step)

            for g in range(NG):
                sp.wait_ge(combined, GROUP * (g + 1))
                cols = slice(g * GROUP * D, (g + 1) * GROUP * D)
                sp.dma_start(out[:, cols], acc[:, g * GROUP:(g + 1) * GROUP, :].rearrange("p j d -> p (j d)"))\
                    .then_inc(out_stored, 16)
            sp.wait_ge(out_stored, 16 * NG)

        @block.gpsimd
        def _(pool):
            pool.memset(zeros[:, :], 0.0).then_inc(zeros_set, 1)
            pool.memset(ident[:, :], 0.0).then_inc(zeros_set, 1)
            pool.memset(eps_tile[:, :], LN_EPS).then_inc(consts_set, 1)
            pool.memset(ones[:, :], 1.0).then_inc(consts_set, 1)
            pool.memset(head_of_row[:, :], 1.0).then_inc(zeros_set, 1)
            pool.memset(earlier[:, :], 1.0).then_inc(zeros_set, 1)
            pool.memset(scan_keep[:, :, :], 1.0).then_inc(zeros_set, 1)
            for i in range(2):
                pool.memset(v_aug[i][:, :, :, VC:AUG], 1.0).then_inc(consts_set, 1)
            pool.wait_ge(zeros_set, 5)
            pool.affine_select(out=ident[:, :], in_=ident[:, :], compare_op=ALU.not_equal, fill=1.0, base=0,
                               pattern=[[-1, P]], channel_multiplier=1).then_inc(ident_set, 1)
            pool.affine_select(out=head_of_row[:, :], in_=head_of_row[:, :], compare_op=ALU.is_ge, fill=0.0, base=0,
                               pattern=[[-HD, HEADS]], channel_multiplier=1).then_inc(zeros_set, 1)
            pool.affine_select(out=earlier[:, :], in_=earlier[:, :], compare_op=ALU.is_ge, fill=0.0, base=-1,
                               pattern=[[1, P]], channel_multiplier=-1).then_inc(consts_set, 1)
            pool.wait_ge(zeros_set, 6)
            pool.affine_select(out=head_of_row[:, :], in_=head_of_row[:, :], compare_op=ALU.is_ge, fill=0.0,
                               base=HD - 1, pattern=[[HD, HEADS]], channel_multiplier=-1).then_inc(ident_set, 1)
            pool.memset(scan_keep[:, :, 0:1], 0.0).then_inc(consts_set, 1)
            pool.iota(rank_of_expert[:, :], pattern=[[-1, E]], base=E, channel_multiplier=0,
                      allow_small_or_imprecise_dtypes=True).then_inc(consts_set, 1)
            pool.iota(tile_number[:, :, :], pattern=[[1, SLOT_TILES], [0, E]], base=0, channel_multiplier=0,
                      allow_small_or_imprecise_dtypes=True).then_inc(consts_set, 1)

            pool.wait_ge(weights_landed, 16 * N_WEIGHTS)
            for g in range(NG):
                tiles = acc[:, g * GROUP:(g + 1) * GROUP, :]
                pool.wait_ge(xn_ready, g + 1)
                pool.tensor_tensor(tiles, tiles, xn[:, g * GROUP:(g + 1) * GROUP, :], ALU.add)\
                    .then_inc(base_added, 1)
                pool.wait_ge(base_added, 2 * g + 1)
                pool.tensor_tensor(tiles, tiles, over_tiles(b_out_sb, GROUP), ALU.add).then_inc(base_added, 1)

            pool.wait_ge(slots_ready, TOPK)
            pool.wait_ge(zeros_landed, 16 * (ST * SLOT_TILES // P // 2))
            for j in range(NT):
                i = routing_tile(j)
                for k in range(TOPK):
                    pool.indirect_dma_start(slots_x, bass.IndirectOffsetOnAxis(slot_i[k][:, i:i + 1], 0),
                                            xn[:, j, :], None).then_inc(scattered, 16)

            pool.wait_ge(y_stored[0], 16 * ((SLOT_TILES + 1) // 2))
            pool.wait_ge(y_stored[1], 16 * (SLOT_TILES // 2))
            for j in range(NT):
                i = routing_tile(j)
                if j >= RING:
                    pool.wait_ge(combined, j - RING + 1)
                for k in range(TOPK):
                    pool.indirect_dma_start(y_back[:, j % RING, k, :], None, slots_y,
                                            bass.IndirectOffsetOnAxis(slot_i[k][:, i:i + 1], 0))\
                        .then_inc(gathered[j % RING], 16)
            for r in range(RING):
                pool.wait_ge(gathered[r], 16 * TOPK * (NT // RING))

        CONSTS = 8

        @block.tensor
        def _(pe):
            pe.wait_ge(weights_landed, 16 * N_WEIGHTS)
            pe.wait_ge(diag_ready, 1)
            diag = proj_diag[:, :, :].rearrange("p h f -> p (h f)")
            pe.matmul(bank[2][:, :], wkT_sb[:, :], diag, start=True, stop=True).then_inc(w_feat_ready, 1)
            pe.matmul(bank[3][:, :], wqT_sb[:, :], diag, start=True, stop=True).then_inc(w_feat_ready, 1)

            def transposes(g):
                if g >= 2:
                    pe.wait_ge(xnT_copied, g - 1)
                pe.wait_ge(xn_ready, g + 1)
                for t in range(GROUP):
                    mm = pe.transpose(bank[g % 2][:, t * P:(t + 1) * P], xn[:, g * GROUP + t, :], ident[:, :])
                mm.then_inc(xnT_ready, 1)

            def router(g):
                pe.wait_ge(xnT_copied, g + 1)
                for t in range(GROUP):
                    j = g * GROUP + t
                    i = routing_tile(j)
                    mm = pe.matmul(bank[ROUTE_BANK][:, i * E:(i + 1) * E], xnT[:, j * P:(j + 1) * P],
                                   router_sb[:, :], start=True, stop=True)
                mm.then_inc(scores_ready, 1)

            pe.wait_ge(ident_set, 1)
            for g in range(NG + 1):
                if g < NG:
                    transposes(g)
                if g >= 1:
                    router(g - 1)

            def xT(f, par, half):
                if isinstance(f, int):
                    return xnT[:, (2 * f + half) * P:(2 * f + half + 1) * P]
                return xT_stage[par][:, half * P:(half + 1) * P]

            def z(n, f, f_half, par):
                if n == 0 and not isinstance(f, int):
                    pe.wait_ge(xT_staged[par], 16 * (f_half + par - ROUTED // 2))
                if late(f, 1):
                    pe.wait_ge(z_shifted, 4 * f + n - 3)
                pe.matmul(bank[Z_BANK + n][:, :], xT(f, par, n % 2),
                          w_feat[:, n // 2, :], start=True, stop=True).then_inc(z_ready, 1)

            def v(f, par):
                if late(f, 1):
                    pe.wait_ge(v_copied, f)
                for h in range(2):
                    mm = pe.matmul(bank[V_BANK][:, h * P:(h + 1) * P], xT(f, par, h),
                                   wv_sb[:, :], start=True, stop=True)
                mm.then_inc(v_ready, 1)

            def kv(b, par):
                pe.wait_ge(feat_ready, 4 * b + 2)
                pe.wait_ge(v_copied, b + 1)
                if late(b, 1):
                    pe.wait_ge(att_ready, b)
                if isinstance(b, int) and b == EARLY:
                    pe.wait_ge(y_copied, SLOT_TILES)
                for c in range(CH):
                    for h in range(2):
                        mm = pe.matmul(bank[KV_BANK][:, c * AUG:(c + 1) * AUG], feat[par][h][:, c * P:(c + 1) * P],
                                       v_aug[par][:, h, c, :], start=(h == 0), stop=(h == 1))
                mm.then_inc(kv_ready, 1)

            def qT(h, b, par):
                pe.wait_ge(feat_ready, 4 * b + 3 + h)
                if h == 1:
                    pe.wait_ge(qT_copied, 2 * b + 1)
                elif late(b, 2):
                    pe.wait_ge(acc_added, b - 1)
                for c in range(CH):
                    mm = pe.transpose(bank[QT_BANK][:, c * P:(c + 1) * P],
                                      feat[par][2 + h][:, c * P:(c + 1) * P], ident[:, :])
                mm.then_inc(qT_ready, 1)

            def numden(b, par):
                pe.wait_ge(qT_copied, 2 * b + 2)
                pe.wait_ge(kv_masked, b + 1)
                for h in range(2):
                    for c in range(CH):
                        at = ND + (h * CH + c) * AUG
                        mm = pe.matmul(bank[KV_BANK][:, at:at + AUG], qT_sb[h][:, c * P:(c + 1) * P],
                                       kv_sb[par][:, c, :], start=True, stop=True)
                mm.then_inc(nd_ready, 1)

            def attention_T(b):
                pe.wait_ge(att_ready, b + 1)
                for h in range(2):
                    mm = pe.transpose(bank[V_BANK][:, (2 + h) * P:(3 + h) * P], att[:, h * P:(h + 1) * P],
                                      ident[:, :])
                mm.then_inc(attT_ready, 1)

            def project(b, last):
                pe.wait_ge(attT_copied, b + 1)
                if not last:
                    pe.wait_ge(qT_copied, 2 * b + 4)
                for h in range(2):
                    mm = pe.matmul(bank[QT_BANK][:, h * P:(h + 1) * P], attT[:, h * P:(h + 1) * P],
                                   w_out_sb[:, :], start=True, stop=True)
                mm.then_inc(proj_ready, 1)

            def route_link(n):
                part = n % 5
                if n >= 5 * SINKHORN_ITERS:
                    if n == 5 * SINKHORN_ITERS + 1:
                        pe.wait_ge(mask_ready, 1)
                        pe.matmul(bank[ROUTE_BANK][:, 0:W], earlier[:, :], mask[:, :], start=True, stop=True)
                        pe.matmul(bank[ROUTE_BANK][:, W:2 * W], ones[:, :], mask[:, :], start=True, stop=True)\
                            .then_inc(counts_ready, 1)
                elif part == 2:
                    pe.wait_ge(row_normed, n // 5 + 1)
                    for h in range(2):
                        mm = pe.transpose(bank[ROUTE_BANK][:, h * P:(h + 1) * P], row_log[:, h * P:(h + 1) * P],
                                          ident[:, :])
                    mm.then_inc(cols_in, 1)
                elif part == 4:
                    pe.wait_ge(col_normed, n // 5 + 1)
                    for h in range(2):
                        mm = pe.transpose(bank[ROUTE_BANK][:, W + h * P:W + (h + 1) * P],
                                          col_log[:, h * P:(h + 1) * P], ident[:, :])
                    mm.then_inc(rows_in, 1)

            def step(b, b_half, par, front=True, back=True, tail=True, route=False):
                f, f_half, f_par = b + 1, b_half + par, 1 - par
                link = 4 * f if route else None
                if front:
                    z(0, f, f_half, f_par)
                if route and link >= 1:
                    route_link(link - 1)
                if front:
                    z(1, f, f_half, f_par)
                if route:
                    route_link(link)
                if back:
                    kv(b, par)
                if front:
                    v(f, f_par)
                if tail:
                    attention_T(b - 1)
                if back:
                    qT(0, b, par)
                if front:
                    z(2, f, f_half, f_par)
                if route:
                    route_link(link + 1)
                if back:
                    qT(1, b, par)
                if front:
                    z(3, f, f_half, f_par)
                if route:
                    route_link(link + 2)
                if tail:
                    project(b - 1, last=not back)
                if back:
                    numden(b, par)

            pe.wait_ge(w_feat_copied, 2)
            attend_early(pe, step)

            def rows_T(k, k_half, par):
                pe.wait_ge(rows_landed[par], 16 * (k_half + 1))
                if late(k, 2):
                    pe.wait_ge(xT_copied, k - 1)
                for t in range(2):
                    mm = pe.transpose(bank[par][:, t * P:(t + 1) * P], x_tile[par][:, t, :], ident[:, :])
                mm.then_inc(xT_ready, 1)

            def up(k, k_half, par):
                pe.wait_ge(xT_copied, k + 1)
                pe.wait_ge(w_up_landed[par], 16 * (k_half + 1))
                if late(k, 2):
                    pe.wait_ge(hidden_ready, k - 1)
                for half in range(2):
                    for c in range(FC):
                        at = half * FF + c * P
                        mm = pe.matmul(bank[2 + 2 * half + par][:, c * ST:(c + 1) * ST], w_up[par][:, at:at + P],
                                       xT_tile[par][:, :], start=True, stop=True)
                    mm.then_inc(up_ready, 1)

            def down(k, k_half, par):
                pe.wait_ge(w_down_landed[par], 16 * (k_half + 1))
                pe.wait_ge(hidden_ready, k + 1)
                if late(k, 2):
                    pe.wait_ge(y_copied, k - 1)
                for t in range(2):
                    for c in range(FC):
                        mm = pe.matmul(bank[6 + par][:, t * D:(t + 1) * D], hidden[par][:, c, t * P:(t + 1) * P],
                                       w_down[par][:, c * D:(c + 1) * D], start=(c == 0), stop=(c == FC - 1))
                mm.then_inc(y_ready, 1)

            def expert_step(k, k_half, par):
                if not isinstance(k, int) or k + 2 < SLOT_TILES:
                    rows_T(k + 2, k_half + 1, par)
                if not isinstance(k, int) or k + 1 < SLOT_TILES:
                    up(k + 1, k_half + par, 1 - par)
                down(k, k_half, par)

            pe.wait_ge(acc_added, EARLY)
            rows_T(0, 0, 0)
            rows_T(1, 0, 1)
            up(0, 0, 0)
            experts(pe, expert_step)
            attend_late(step)

        @block.scalar
        def _(act):
            for dst, src in ((router_sb[:, :], router_wT), (wkT_sb[:, :], wkT), (wqT_sb[:, :], wqT),
                             (proj_sb[:, :], proj), (wv_sb[:, :], wv), (w_out_sb[:, :], w_out),
                             (b_out_sb[:, :], b_out.broadcast_to([P, D])),
                             (router_b_sb[:, :], router_b.broadcast_to([P, E])),
                             (temp_sb[:, :], temperature.broadcast_to([P, 1]))):
                act.dma_start(dst, src).then_inc(weights_landed, 16)

            act.wait_ge(consts_set, CONSTS)

            def root(g):
                act.wait_ge(moments_done, g + 1)
                tiles = slice(g * GROUP, (g + 1) * GROUP)
                act.activation(std[:, tiles], moments[:, tiles, 1], ACT.Sqrt, bias=eps_tile[:, :])\
                    .then_inc(std_done, 1)

            def copy_xnT(g):
                act.wait_ge(xnT_ready, g + 1)
                act.copy(xnT[:, g * GROUP * P:(g + 1) * GROUP * P], bank[g % 2][:, :]).then_inc(xnT_copied, 1)

            for g in range(NG + 2):
                if g < NG:
                    root(g)
                if g >= 2:
                    copy_xnT(g - 2)
            act.preload_act_table_set(EXP_LN_TABLE)
            for n in range(2):
                act.wait_ge(w_feat_ready, n + 1)
                act.copy(w_feat[:, n, :], bank[2 + n][:, :]).then_inc(w_feat_copied, 1)

            def features(n, f, par):
                act.wait_ge(z_shifted, 4 * f + n + 1)
                if late(f, 2):
                    if n < 2:
                        act.wait_ge(kv_ready, f - 1)
                    else:
                        act.wait_ge(qT_ready, 2 * f - 4 + n - 1)
                act.activation(feat[par][n][:, :], z_sb[n][:, :], ACT.Exp).then_inc(feat_ready, 1)

            def copy_v(f, par):
                act.wait_ge(v_ready, f + 1)
                if late(f, 2):
                    act.wait_ge(kv_ready, f - 1)
                act.copy(v_aug[par][:, :, :, 0:VC], bank[V_BANK][:, 0:2 * P]
                         .rearrange("p (h c v) -> p h c v", h=2, c=CH)).then_inc(v_copied, 1)

            def copy_qT(h, b):
                act.wait_ge(qT_ready, 2 * b + h + 1)
                if late(b, 1):
                    act.wait_ge(nd_ready, b)
                act.copy(qT_sb[h][:, :], bank[QT_BANK][:, :]).then_inc(qT_copied, 1)

            def copy_attT(b):
                act.wait_ge(attT_ready, b + 1)
                if late(b, 1):
                    act.wait_ge(proj_ready, b)
                act.copy(attT[:, :], bank[V_BANK][:, 2 * P:4 * P]).then_inc(attT_copied, 1)

            def route_link(n):
                it, part = n // 5, n % 5
                if n == 5 * SINKHORN_ITERS:
                    act.wait_ge(rows_in, SINKHORN_ITERS)
                    act.activation(gate_exp[:, :], bank[ROUTE_BANK][:, W:2 * W], ACT.Exp).then_inc(gates_exped, 1)
                elif n < 5 * SINKHORN_ITERS:
                    if part == 0:
                        act.wait_ge(row_shifted, it + 1)
                        act.activation(row_exp[:, :], row_shift[:, :], ACT.Exp).then_inc(row_exped, 1)
                    elif part == 1:
                        act.wait_ge(row_summed, it + 1)
                        act.activation(row_ln[:, :], row_sum[:, :], ACT.Ln).then_inc(row_lned, 1)
                    elif part == 3:
                        act.wait_ge(col_maxed, it + 1)
                        act.activation(col_exp[:, :], bank[ROUTE_BANK][:, 0:W], ACT.Exp, bias=col_negmax[:, :],
                                       accum_out=col_sum[:, :]).then_inc(col_summed, 1)
                        act.wait_ge(col_summed, it + 1)
                        act.activation(col_ln[:, :], col_sum[:, :], ACT.Ln).then_inc(col_lned, 1)

            def step(b, b_half, par, front=True, back=True, tail=True, route=False):
                f, f_par = b + 1, 1 - par
                link = 4 * f if route else None
                if front:
                    features(0, f, f_par)
                if route:
                    route_link(link)
                if front:
                    features(1, f, f_par)
                if route:
                    route_link(link + 1)
                if tail:
                    copy_attT(b - 1)
                if front:
                    copy_v(f, f_par)
                if back:
                    copy_qT(0, b)
                    copy_qT(1, b)
                if front:
                    features(2, f, f_par)
                if route:
                    route_link(link + 2)
                if front:
                    features(3, f, f_par)
                if route:
                    route_link(link + 3)

            attend_early(act, step)

            def copy_xT(k, par):
                act.wait_ge(xT_ready, k + 1)
                if late(k, 2):
                    act.wait_ge(up_ready, 2 * k - 2)
                act.copy(xT_tile[par][:, :], bank[par][:, 0:ST]).then_inc(xT_copied, 1)

            def relu(k, par):
                act.wait_ge(up_ready, 2 * k + 1)
                if late(k, 2):
                    act.wait_ge(hidden_ready, k - 1)
                act.activation(gate_act[par][:, :], bank[2 + par][:, :], ACT.Relu).then_inc(relu_done, 1)

            def expert_step(k, k_half, par):
                if not isinstance(k, int) or k + 2 < SLOT_TILES:
                    copy_xT(k + 2, par)
                if not isinstance(k, int) or k + 1 < SLOT_TILES:
                    relu(k + 1, 1 - par)

            copy_xT(0, 0)
            copy_xT(1, 1)
            relu(0, 0)
            experts(act, expert_step)
            attend_late(step)

        @block.vector
        def _(dve):
            dve.memset(chunk_mask[:, :], 0.0).then_inc(chunk_mask_set, 1)
            dve.wait_ge(chunk_mask_set, 1)
            for m in range(HC):
                rows = slice(F * m, F * (m + 1))
                dve.memset(chunk_mask[rows, HD * m:HD * (m + 1)], 1.0).then_inc(chunk_mask_set, 1)
                dve.memset(chunk_mask[rows, VC + m:VC + m + 1], 1.0).then_inc(chunk_mask_set, 1)

            def statistics(g):
                dve.wait_ge(x_landed[g], 16)
                for t in range(GROUP):
                    ins = dve.bn_stats(stats[:, g * GROUP + t, :], acc[:, g * GROUP + t, :])
                ins.then_inc(stats_done, 1)
                dve.wait_ge(stats_done, g + 1)
                for t in range(GROUP):
                    ins = dve.bn_aggr(moments[:, g * GROUP + t, :], stats[:, g * GROUP + t, :])
                ins.then_inc(moments_done, 1)

            def normalise(g):
                tiles = slice(g * GROUP, (g + 1) * GROUP)
                dve.wait_ge(std_done, g + 1)
                dve.reciprocal(rstd[:, tiles], std[:, tiles]).then_inc(rstd_done, 1)
                dve.wait_ge(rstd_done, g + 1)
                for t in range(GROUP):
                    j = g * GROUP + t
                    ins = dve.tensor_scalar(xn[:, j, :], acc[:, j, :], moments[:, j, 0:1], rstd[:, j:j + 1],
                                            ALU.subtract, ALU.mult)
                ins.then_inc(xn_ready, 1)

            for g in range(NG + 1):
                if g < NG:
                    statistics(g)
                if g >= 1:
                    normalise(g - 1)
                if g == 1:
                    dve.wait_ge(weights_landed, 16 * N_WEIGHTS)
                    dve.wait_ge(ident_set, 2)
                    dve.tensor_tensor(proj_diag[:, :, :], over_tiles(proj_sb, HEADS), wide(head_of_row, F), ALU.mult)\
                        .then_inc(diag_ready, 1)

            def z(n, f):
                args = bank[Z_BANK + n][:, :].rearrange("p (h f) -> p h f", f=F)
                dve.wait_ge(z_ready, 4 * f + n + 1)
                dve.tensor_reduce(neg_max[n][:, :], args, AX_X, ALU.max, negate=True).then_inc(z_negmax, 1)
                dve.wait_ge(z_negmax, 4 * f + n + 1)
                if late(f, 1):
                    dve.wait_ge(feat_ready, 4 * f + n - 3)
                dve.tensor_tensor(z_sb[n][:, :].rearrange("p (h f) -> p h f", f=F), args, wide(neg_max[n], F), ALU.add)\
                    .then_inc(z_shifted, 1)

            def mask_kv(b, par):
                dve.wait_ge(kv_ready, b + 1)
                if late(b, 2):
                    dve.wait_ge(nd_ready, b - 1)
                dve.tensor_tensor(kv_sb[par][:, :, :], bank[KV_BANK][:, 0:CH * AUG].rearrange("p (c a) -> p c a", c=CH),
                                  over_tiles(chunk_mask, CH), ALU.mult).then_inc(kv_masked, 1)

            def divide(b):
                nd = bank[KV_BANK][:, ND:ND + 2 * CH * AUG].rearrange("p (c a) -> p c a", a=AUG)
                dve.wait_ge(nd_ready, b + 1)
                dve.tensor_scalar(den[:, :, :], nd[:, :, VC:AUG], DEN_EPS, None, ALU.add).then_inc(den_step, 1)
                dve.wait_ge(den_step, 2 * b + 1)
                dve.reciprocal(inv_den[:, :, :], den[:, :, :]).then_inc(den_step, 1)
                dve.wait_ge(den_step, 2 * b + 2)
                if late(b, 1):
                    dve.wait_ge(attT_ready, b)
                dve.tensor_tensor(att[:, :].rearrange("p (c m d) -> p c m d", c=2 * CH, m=HC),
                                  nd[:, :, 0:VC].rearrange("p c (m d) -> p c m d", m=HC),
                                  inv_den[:, :, :].unsqueeze(3).broadcast_to([P, 2 * CH, HC, HD]), ALU.mult)\
                    .then_inc(att_ready, 1)

            def add_projection(b):
                dve.wait_ge(proj_ready, b + 1)
                tiles = acc[:, bass.ds(2 * b, 2), :]
                dve.tensor_tensor(tiles, bank[QT_BANK][:, 0:2 * P].rearrange("p (t d) -> p t d", t=2), tiles, ALU.add)\
                    .then_inc(acc_added, 1)

            own = [0]

            def settle(ins):
                own[0] += 1
                ins.then_inc(route_step, 1)
                dve.wait_ge(route_step, own[0])

            def choose(k, values):
                settle(dve.tensor_reduce(top[k][:, :], by_tile(values), AX_X, ALU.max))
                settle(dve.tensor_tensor(by_tile(is_best), by_tile(values), wide(top[k], E), ALU.is_equal))
                settle(dve.tensor_tensor(by_tile(ranked), by_tile(is_best), over_tiles(rank_of_expert, NT), ALU.mult))
                settle(dve.tensor_reduce(best_rank[:, :], by_tile(ranked), AX_X, ALU.max))
                settle(dve.tensor_tensor(by_tile(chosen[k]), by_tile(ranked), wide(best_rank, E), ALU.is_equal))

            def route_link(n):
                it, part = n // 5, n % 5
                if n < 5 * SINKHORN_ITERS:
                    if part == 0:
                        if it == 0:
                            src = scores[:, :]
                        else:
                            dve.wait_ge(rows_in, it)
                            src = bank[ROUTE_BANK][:, W:2 * W]
                        src = src.rearrange("p (i e) -> p i e", e=E)
                        settle(dve.tensor_reduce(row_max[:, :], src, AX_X, ALU.max))
                        dve.tensor_tensor(by_tile(row_shift), src, wide(row_max, E), ALU.subtract)\
                            .then_inc(row_shifted, 1)
                    elif part == 1:
                        dve.wait_ge(row_exped, it + 1)
                        dve.tensor_reduce(row_sum[:, :], by_tile(row_exp), AX_X, ALU.add).then_inc(row_summed, 1)
                    elif part == 2:
                        dve.wait_ge(row_lned, it + 1)
                        dve.tensor_tensor(by_tile(row_log), by_tile(row_shift), wide(row_ln, E), ALU.subtract)\
                            .then_inc(row_normed, 1)
                    elif part == 3:
                        dve.wait_ge(cols_in, it + 1)
                        dve.tensor_reduce(col_negmax[:, :], bank[ROUTE_BANK][:, 0:W], AX_X, ALU.max, negate=True)\
                            .then_inc(col_maxed, 1)
                    elif part == 4:
                        dve.wait_ge(col_lned, it + 1)
                        dve.tensor_scalar(col_log[:, :], bank[ROUTE_BANK][:, 0:W], col_negmax[:, :], col_ln[:, :],
                                          ALU.add, ALU.subtract).then_inc(col_normed, 1)
                elif n == 5 * SINKHORN_ITERS:
                    dve.wait_ge(gates_exped, 1)
                    settle(dve.tensor_reduce(gate_sum[:, :], by_tile(gate_exp), AX_X, ALU.add))
                    settle(dve.tensor_scalar(gate_sum[:, :], gate_sum[:, :], GATE_EPS, None, ALU.add))
                    settle(dve.reciprocal(gate_inv[:, :], gate_sum[:, :]))
                    settle(dve.tensor_tensor(by_tile(gates), by_tile(gate_exp), wide(gate_inv, E), ALU.mult))
                    choose(0, gates)
                elif n == 5 * SINKHORN_ITERS + 1:
                    settle(dve.scalar_tensor_tensor(rest[:, :], chosen[0][:, :], -4.0, gates[:, :], ALU.mult, ALU.add))
                    choose(1, rest)
                    dve.tensor_tensor(mask[:, :], chosen[0][:, :], chosen[1][:, :], ALU.add).then_inc(mask_ready, 1)
                elif n == 5 * SINKHORN_ITERS + 2:
                    settle(dve.tensor_tensor(top_sum[:, :], top[0][:, :], top[1][:, :], ALU.add))
                    settle(dve.tensor_scalar(top_sum[:, :], top_sum[:, :], GATE_EPS, None, ALU.add))
                    settle(dve.reciprocal(top_inv[:, :], top_sum[:, :]))
                    for k in range(TOPK):
                        settle(dve.tensor_tensor(weight[k][:, :], top[k][:, :], top_inv[:, :], ALU.mult))
                elif n == 5 * SINKHORN_ITERS + 3:
                    place()

            def place():
                dve.wait_ge(counts_ready, 1)
                settle(dve.tensor_copy(totals[:, :, :].rearrange("p e i -> p i e"),
                                       bank[ROUTE_BANK][:, W:2 * W].rearrange("p (i e) -> p i e", e=E)))
                settle(dve.tensor_tensor_scan(prefix[:, :, :].rearrange("p e i -> p (e i)"),
                                              scan_keep[:, :, :].rearrange("p e i -> p (e i)"),
                                              totals[:, :, :].rearrange("p e i -> p (e i)"), 0.0, ALU.mult, ALU.add))
                settle(dve.tensor_scalar(padded_i[:, :], prefix[:, :, NT - 1], float(ST - 1), None, ALU.add))
                settle(dve.tensor_scalar(tiles_i[:, :], padded_i[:, :], ST.bit_length() - 1, None,
                                         ALU.logical_shift_right))
                settle(dve.tensor_copy(tiles_f[:, :], tiles_i[:, :]))
                settle(dve.tensor_tensor_scan(tiles_end[:, :], ones[:, 0:E], tiles_f[:, :], 0.0, ALU.mult, ALU.add))
                settle(dve.tensor_tensor(first_slot[:, :], tiles_end[:, :], tiles_f[:, :], ALU.subtract))
                settle(dve.tensor_scalar(first_slot[:, :], first_slot[:, :], float(ST), None, ALU.mult))
                settle(dve.tensor_tensor(start[:, :, :], prefix[:, :, :], totals[:, :, :], ALU.subtract))
                settle(dve.tensor_tensor(start[:, :, :], start[:, :, :], wide(first_slot, NT), ALU.add))
                settle(dve.tensor_tensor(by_tile(position), bank[ROUTE_BANK][:, 0:W].rearrange("p (i e) -> p i e", e=E),
                                         start[:, :, :].rearrange("p e i -> p i e"), ALU.add))
                for k in range(TOPK):
                    settle(dve.tensor_tensor(picked[k][:, :], chosen[k][:, :], position[:, :], ALU.mult))
                    settle(dve.tensor_reduce(slot_f[k][:, :], by_tile(picked[k]), AX_X, ALU.add))
                    dve.tensor_copy(slot_i[k][:, :], slot_f[k][:, :]).then_inc(slots_ready, 1)
                settle(dve.tensor_tensor(past[:, :, :], tile_number[:, :, :], over_tiles(tiles_end, SLOT_TILES), ALU.is_ge))
                settle(dve.tensor_reduce(expert_f[:, :], past[:, :, :], AX_X, ALU.add))
                dve.tensor_scalar(expert_i[:, :], expert_f[:, :], float(E - 1), None, ALU.min).then_inc(experts_ready, 1)

            def step(b, b_half, par, front=True, back=True, tail=True, route=False):
                f = b + 1
                link = 4 * f if route else None
                if tail:
                    divide(b - 1)
                if front:
                    z(0, f)
                if route:
                    route_link(link)
                if front:
                    z(1, f)
                if route:
                    route_link(link + 1)
                if back:
                    mask_kv(b, par)
                if front:
                    z(2, f)
                if route:
                    route_link(link + 2)
                if front:
                    z(3, f)
                if route:
                    route_link(link + 3)
                if tail:
                    add_projection(b - 1)

            dve.wait_ge(chunk_mask_set, 1 + 2 * HC)
            dve.wait_ge(consts_set, CONSTS)
            settle(dve.tensor_scalar(temp_lim[:, :], temp_sb[:, :], 0.1, None, ALU.max))
            settle(dve.reciprocal(inv_temp[:, :], temp_lim[:, :]))
            dve.wait_ge(scores_ready, NG)
            settle(dve.tensor_tensor(by_tile(scores), bank[ROUTE_BANK][:, 0:W].rearrange("p (i e) -> p i e", e=E),
                                     over_tiles(router_b_sb, NT), ALU.add))
            settle(dve.tensor_scalar(scores[:, :], scores[:, :], inv_temp[:, :], None, ALU.mult))
            dve.wait_ge(base_added, 2 * NG)
            attend_early(dve, step)

            def multiply(k, par):
                dve.wait_ge(relu_done, k + 1)
                dve.wait_ge(up_ready, 2 * k + 2)
                if late(k, 2):
                    dve.wait_ge(y_ready, k - 1)
                dve.tensor_tensor(hidden[par][:, :, :].rearrange("p c s -> p (c s)"), bank[4 + par][:, :],
                                  gate_act[par][:, :], ALU.mult).then_inc(hidden_ready, 1)

            def copy_y(k, k_half, par):
                dve.wait_ge(y_ready, k + 1)
                if late(k, 2):
                    dve.wait_ge(y_stored[par], 16 * k_half)
                dve.tensor_copy(y_tile[par][:, :, :].rearrange("p t d -> p (t d)"), bank[6 + par][:, 0:2 * D])\
                    .then_inc(y_copied, 1)

            def expert_step(k, k_half, par):
                if not isinstance(k, int) or k + 1 < SLOT_TILES:
                    multiply(k + 1, 1 - par)
                copy_y(k, k_half, par)

            multiply(0, 0)
            experts(dve, expert_step)

            def add_row(j, k, done):
                i = routing_tile(j)
                dve.scalar_tensor_tensor(acc[:, j, :], y_back[:, j % RING, k, :], weight[k][:, i:i + 1],
                                         acc[:, j, :], ALU.mult, ALU.add).then_inc(done, 1)

            def combine(g):
                tiles = range(g * GROUP, (g + 1) * GROUP)
                dve.wait_ge(acc_added, (g + 1) * GROUP // 2)
                for j in tiles:
                    dve.wait_ge(gathered[j % RING], 16 * TOPK * (j // RING + 1))
                    add_row(j, 0, first_added)
                for j in tiles:
                    dve.wait_ge(first_added, j + 1)
                    add_row(j, 1, combined)

            def late_step(b, b_half, par, front, back, tail):
                step(b, b_half, par, front=front, back=back, tail=tail)
                if b >= EARLY:
                    combine(b - EARLY)

            attend_late(late_step)
            for g in range(NB + 1 - EARLY, NG):
                combine(g)


def kernel(L0_attn_x, L0_attn_w_qkv, L0_attn_w_out, L0_attn_b_out, L0_attn_proj, L0_ffn_router_w, L0_ffn_router_b,
           L0_ffn_temperature, L0_ffn_wg, L0_ffn_wp, L0_ffn_wo):
    import numpy as np
    import concourse.bacc as bacc
    from concourse.bass_utils import run_bass_kernel_spmd

    x = np.asarray(L0_attn_x)
    B, T, D = x.shape
    NT = B * T // P
    w_qkv = np.asarray(L0_attn_w_qkv)
    wg, wp, wo = (np.asarray(a) for a in (L0_ffn_wg, L0_ffn_wp, L0_ffn_wo))
    E, _, FF = wg.shape
    wo_rows = wo.reshape(E, FF // P, P, D).transpose(0, 2, 1, 3).reshape(E, P, FF // P * D)
    arrays = {
        "x_dram": x.reshape(NT, P, D).transpose(1, 0, 2).reshape(P, NT * D),
        "wqT_dram": w_qkv[:, 0:D].T,
        "wkT_dram": w_qkv[:, D:2 * D].T,
        "wv_dram": w_qkv[:, 2 * D:3 * D],
        "w_out_dram": np.asarray(L0_attn_w_out),
        "b_out_dram": np.asarray(L0_attn_b_out).reshape(1, D),
        "proj_dram": np.asarray(L0_attn_proj).reshape(D, -1),
        "router_wT_dram": np.asarray(L0_ffn_router_w).T,
        "router_b_dram": np.asarray(L0_ffn_router_b).reshape(1, E),
        "temperature_dram": np.asarray(L0_ffn_temperature).reshape(1, 1),
        "w_expert_dram": np.concatenate([wg, wp, wo_rows], axis=2),
    }
    arrays = {n: np.ascontiguousarray(a) for n, a in arrays.items()}
    nc = bacc.Bacc("TRN2", target_bir_lowering=False, num_devices=1)
    args = [nc.dram_tensor(n, a.shape, mybir.dt.from_np(a.dtype), kind="ExternalInput").ap() for n, a in arrays.items()]
    out = nc.dram_tensor("out_dram", (P, NT * D), F32, kind="ExternalOutput").ap()
    build_program(nc, *args, out)
    r = run_bass_kernel_spmd(nc, [arrays], core_ids=[0])
    got = np.asarray(r.results[0]["out_dram"])
    return got.reshape(P, NT, D).transpose(1, 0, 2).reshape(B, T, D)
```

```python
from contextlib import ExitStack

import concourse.bass as bass
from concourse import mybir

F32 = mybir.dt.float32
I32 = mybir.dt.int32
ALU = mybir.AluOpType
ACT = mybir.ActivationFunctionType
AX_X = mybir.AxisListType.X

P = 128
LN_EPS = 1e-5
DEN_EPS = 1e-6
GATE_EPS = 1e-8
SINKHORN_ITERS = 3
SQRT_TABLE = "sqrt_and_others"
EXP_LN_TABLE = "natural_log_exp_and_others"


def build_program(nc, x, wqT, wkT, wv, w_out, b_out, proj, router_wT, router_b, temperature, w_expert, out):
    D = wv.shape[0]
    NT = x.shape[1] // D
    NB = NT // 2
    HEADS, F = 16, proj.shape[1]
    HD = D // HEADS
    E = router_wT.shape[1]
    FF = w_expert.shape[2] // 3
    FC = FF // P
    FEAT = HEADS * F
    CH = FEAT // P
    HC = HEADS // CH
    VC = HC * HD
    AUG = VC + HC
    TOPK = 2
    ST = 256
    SLOT_TILES = (NT * P * TOPK - E) // ST + E
    GROUP = 4
    NG = NT // GROUP
    RING = 8
    BY_ACT = 2
    ROUTED = 2
    LINKS = 8
    EARLY = 8

    slots_x = nc.dram_tensor("slots_x", [SLOT_TILES * ST, D], F32, kind="Internal").ap()
    slots_y = nc.dram_tensor("slots_y", [SLOT_TILES * ST, D], F32, kind="Internal").ap()

    with ExitStack() as ctx:
        def sb(name, shape, dt=F32):
            return ctx.enter_context(nc.sbuf_tensor(name, shape, dt))

        def sem(name):
            return ctx.enter_context(nc.semaphore(name))

        ident = sb("ident", [P, P])
        ones = sb("ones", [P, P])
        earlier = sb("earlier", [P, P])
        head_of_row = sb("head_of_row", [P, HEADS])
        chunk_mask = sb("chunk_mask", [P, AUG])
        rank_of_expert = sb("rank_of_expert", [P, E])
        tile_number = sb("tile_number", [P, SLOT_TILES, E])
        scan_keep = sb("scan_keep", [P, E, NT])
        eps_tile = sb("eps_tile", [P, 1])
        zeros = sb("zeros", [P, 2 * D])

        acc = sb("acc", [P, NT, D])
        xn = sb("xn", [P, NT, D])
        xnT = sb("xnT", [P, NT * P])
        wqT_sb, wkT_sb, wv_sb, w_out_sb = (sb(n, [P, D]) for n in ("wqT_sb", "wkT_sb", "wv_sb", "w_out_sb"))
        b_out_sb = sb("b_out_sb", [P, D])
        proj_sb = sb("proj_sb", [P, F])
        proj_diag = sb("proj_diag", [P, HEADS, F])
        w_feat = sb("w_feat", [P, 2, FEAT])
        router_sb = sb("router_sb", [P, E])
        router_b_sb = sb("router_b_sb", [P, E])
        temp_sb = sb("temp_sb", [P, 1])
        temp_lim = sb("temp_lim", [P, 1])
        inv_temp = sb("inv_temp", [P, 1])
        stats = sb("stats", [P, NT, 6])
        moments = sb("moments", [P, NT, 2])
        std = sb("std", [P, NT])
        rstd = sb("rstd", [P, NT])
        shift = sb("shift", [P, NT])

        xT_stage = [sb(f"xT_stage{i}", [P, 2 * P]) for i in range(2)]
        v_aug = [sb(f"v_aug{i}", [P, 2, CH, AUG]) for i in range(2)]
        neg_max = [sb(f"neg_max{n}", [P, HEADS]) for n in range(4)]
        z_sb = [sb(f"z_sb{n}", [P, FEAT]) for n in range(4)]
        feat = [[sb(f"feat{i}_{n}", [P, FEAT]) for n in range(4)] for i in range(2)]
        kv_sb = [sb(f"kv_sb{i}", [P, CH, AUG]) for i in range(2)]
        qT_sb = [sb(f"qT_sb{h}", [P, CH * P]) for h in range(2)]
        den = sb("den", [P, 2 * CH, HC])
        inv_den = sb("inv_den", [P, 2 * CH, HC])
        att = sb("att", [P, 2 * P])
        attT = sb("attT", [P, 2 * P])

        W = NT * E
        scores = sb("scores", [P, W])
        row_max, row_sum, row_ln = (sb(n, [P, NT]) for n in ("row_max", "row_sum", "row_ln"))
        row_shift, row_exp, row_log = (sb(n, [P, W]) for n in ("row_shift", "row_exp", "row_log"))
        col_negmax, col_sum, col_ln = (sb(n, [P, 1]) for n in ("col_negmax", "col_sum", "col_ln"))
        col_exp, col_log = (sb(n, [P, 2 * P]) for n in ("col_exp", "col_log"))
        gate_exp, gates, rest = (sb(n, [P, W]) for n in ("gate_exp", "gates", "rest"))
        gate_sum, gate_inv, best_rank = (sb(n, [P, NT]) for n in ("gate_sum", "gate_inv", "best_rank"))
        top = [sb(f"top{k}", [P, NT]) for k in range(TOPK)]
        chosen = [sb(f"chosen{k}", [P, W]) for k in range(TOPK)]
        is_best, ranked, mask = (sb(n, [P, W]) for n in ("is_best", "ranked", "mask"))
        top_sum, top_inv = sb("top_sum", [P, NT]), sb("top_inv", [P, NT])
        weight = [sb(f"weight{k}", [P, NT]) for k in range(TOPK)]
        totals, prefix, start = (sb(n, [P, E, NT]) for n in ("totals", "prefix", "start"))
        position, picked = sb("position", [P, W]), [sb(f"picked{k}", [P, W]) for k in range(TOPK)]
        padded_i, tiles_i = sb("padded_i", [P, E], I32), sb("tiles_i", [P, E], I32)
        tiles_f, tiles_end, first_slot = (sb(n, [P, E]) for n in ("tiles_f", "tiles_end", "first_slot"))
        slot_f = [sb(f"slot_f{k}", [P, NT]) for k in range(TOPK)]
        slot_i = [sb(f"slot_i{k}", [P, NT], I32) for k in range(TOPK)]
        past = sb("past", [P, SLOT_TILES, E])
        expert_f = sb("expert_f", [P, SLOT_TILES])
        expert_i = sb("expert_i", [P, SLOT_TILES], I32)

        w_tile = [sb(f"w_tile{i}", [P, 3 * FF]) for i in range(4)]
        x_tile = [sb(f"x_tile{i}", [P, 2, D]) for i in range(2)]
        xT_tile = [sb(f"xT_tile{i}", [P, ST]) for i in range(2)]
        gate_act = [sb(f"gate_act{i}", [P, FC * ST]) for i in range(2)]
        hidden = [sb(f"hidden{i}", [P, FC, ST]) for i in range(2)]
        y_tile = [sb(f"y_tile{i}", [P, 2, D]) for i in range(2)]
        y_back = sb("y_back", [P, RING, TOPK, D])

        bank = [ctx.enter_context(nc.psum_tensor(f"bank{i}", [P, 512], F32)) for i in range(8)]
        V_BANK, Z_BANK, QT_BANK, KV_BANK, ROUTE_BANK = 0, 1, 5, 6, 7
        ND = CH * AUG

        x_landed = [sem(f"x_landed{g}") for g in range(NG)]
        feature_weights_landed, weights_landed, zeros_landed = (
            sem(n) for n in ("feature_weights_landed", "weights_landed", "zeros_landed"))
        zeros_set, consts_set, ident_set, chunk_mask_set = (
            sem(n) for n in ("zeros_set", "consts_set", "ident_set", "chunk_mask_set"))
        stats_done, moments_done, std_done, rstd_done, shift_done = (
            sem(n) for n in ("stats_done", "moments_done", "std_done", "rstd_done", "shift_done"))
        xn_by_dve, xn_by_act = sem("xn_by_dve"), sem("xn_by_act")
        xnT_ready, xnT_copied, scores_ready, base_added = (
            sem(n) for n in ("xnT_ready", "xnT_copied", "scores_ready", "base_added"))
        diag_ready, w_feat_ready, w_feat_copied = sem("diag_ready"), sem("w_feat_ready"), sem("w_feat_copied")
        xT_staged = [sem(f"xT_staged{i}") for i in range(2)]
        z_ready, z_negmax, z_shifted, feat_ready = (
            sem(n) for n in ("z_ready", "z_negmax", "z_shifted", "feat_ready"))
        v_ready, v_copied, kv_ready, kv_masked = (sem(n) for n in ("v_ready", "v_copied", "kv_ready", "kv_masked"))
        qT_ready, qT_copied, nd_ready, den_step, att_ready = (
            sem(n) for n in ("qT_ready", "qT_copied", "nd_ready", "den_step", "att_ready"))
        attT_ready, attT_copied, proj_ready, acc_added = (
            sem(n) for n in ("attT_ready", "attT_copied", "proj_ready", "acc_added"))
        route_step = sem("route_step")
        row_shifted, row_exped, row_summed, row_lned, row_normed = (
            sem(n) for n in ("row_shifted", "row_exped", "row_summed", "row_lned", "row_normed"))
        cols_in, col_maxed, col_summed, col_lned, col_normed, rows_in = (
            sem(n) for n in ("cols_in", "col_maxed", "col_summed", "col_lned", "col_normed", "rows_in"))
        gates_exped, mask_ready, counts_ready, slots_ready, experts_ready = (
            sem(n) for n in ("gates_exped", "mask_ready", "counts_ready", "slots_ready", "experts_ready"))
        scattered = sem("scattered")
        w_landed = [sem(f"w_landed{i}") for i in range(4)]
        rows_landed = [sem(f"rows_landed{i}") for i in range(2)]
        y_stored = [sem(f"y_stored{i}") for i in range(2)]
        xT_ready, xT_copied, up_ready, relu_done, hidden_ready, y_ready, y_copied = (
            sem(n) for n in ("xT_ready", "xT_copied", "up_ready", "relu_done", "hidden_ready", "y_ready", "y_copied"))
        gathered = [sem(f"gathered{i}") for i in range(RING)]
        row_added = [sem(f"row{k}_added") for k in range(TOPK)]
        out_stored = sem("out_stored")

        N_FEATURE_WEIGHTS, N_WEIGHTS = 4, 5

        def routing_tile(j):
            return (j % 2) * NB + j // 2

        def by_tile(t):
            return t[:, :].rearrange("p (i e) -> p i e", e=E)

        def wide(t, n):
            return t[:, :].unsqueeze(2).broadcast_to([P, t.shape[1], n])

        def over_tiles(t, n):
            return t[:, :].unsqueeze(1).broadcast_to([P, n, t.shape[1]])

        def late(v, n):
            return not isinstance(v, int) or v >= n

        def attend_early(engine, step):
            step(-1, -1, 1, back=False, tail=False, route=True)
            step(0, 0, 0, tail=False, route=True)
            for b in range(1, ROUTED):
                step(b, b // 2, b % 2, route=True)
            with engine.Fori(ROUTED // 2, EARLY // 2) as i:
                step(2 * i, i, 0)
                step(2 * i + 1, i, 1)

        def attend_late(step):
            for b in range(EARLY, NB + 1):
                step(b, b // 2, b % 2, front=b + 1 < NB, back=b < NB)

        def ahead(n, q, r):
            return 4 * q + r + n, q + (r + n) // 4, (r + n) % 4

        def exists(k):
            return not isinstance(k, int) or k < SLOT_TILES

        def experts(engine, step):
            for k in range(4):
                step(k // 4, k % 4)
            last = (SLOT_TILES - 4) // 4
            with engine.Fori(1, last) as q:
                for r in range(4):
                    step(q, r)
            for k in range(4 * last, SLOT_TILES):
                step(k // 4, k % 4)

        block = ctx.enter_context(nc.Block())

        @block.sync
        def _(sp):
            for g in range(NG):
                cols = slice(g * GROUP * D, (g + 1) * GROUP * D)
                sp.dma_start(acc[:, g * GROUP:(g + 1) * GROUP, :].rearrange("p j d -> p (j d)"),
                             x[:, cols]).then_inc(x_landed[g], 16)
            for dst, src in ((wv_sb[:, :], wv), (w_out_sb[:, :], w_out), (b_out_sb[:, :], b_out.broadcast_to([P, D])),
                             (router_b_sb[:, :], router_b.broadcast_to([P, E])),
                             (temp_sb[:, :], temperature.broadcast_to([P, 1]))):
                sp.dma_start(dst, src).then_inc(weights_landed, 16)
            sp.wait_ge(zeros_set, 1)
            ZR = ST * SLOT_TILES // P
            for r in range(0, ZR, 2):
                rows = slots_x.rearrange("(p r) d -> p (r d)", p=P)
                sp.dma_start(rows[:, r * D:(r + 2) * D], zeros[:, :]).then_inc(zeros_landed, 16)

            def stage(f_half, par):
                f = 2 * f_half + par
                sp.wait_ge(z_ready, 4 * (f - 1))
                sp.wait_ge(v_ready, f - 1)
                cols = bass.ds(f * (2 * P), 2 * P)
                sp.dma_start(xT_stage[par][:, :], xnT[:, cols]).then_inc(xT_staged[par], 16)

            sp.wait_ge(xnT_copied, NG)
            with sp.Fori(ROUTED // 2, EARLY // 2) as i:
                stage(i, 1)
                stage(i + 1, 0)

            expert_reg = sp.alloc_register("expert_reg")
            ys = slots_y.rearrange("(k t p) d -> k p t d", t=2, p=P)
            xs = slots_x.rearrange("(k t p) d -> k p t d", t=2, p=P)

            def load_rows(k, q, r):
                if late(k, 2):
                    sp.wait_ge(xT_ready, k - 1)
                sp.dma_start(x_tile[r % 2][:, :, :],
                             xs[bass.ds(k, 1), :, :, :].rearrange("a p t d -> (a p) t d"))\
                    .then_inc(rows_landed[r % 2], 16)

            def load_weights(k, q, r):
                sp.reg_load(expert_reg, expert_i[0:1, bass.ds(k, 1)])
                e = bass.ds(sp.snap(expert_reg, min_val=0, max_val=E - 1), 1)
                if late(k, 4):
                    sp.wait_ge(y_ready, k - 3)
                sp.dma_start(w_tile[r][:, :], w_expert[e, :, :].rearrange("a p n -> (a p) n"))\
                    .then_inc(w_landed[r], 16)

            def store_tile(k, q, r):
                sp.wait_ge(y_copied, k + 1)
                sp.dma_start(ys[bass.ds(k, 1), :, :, :].rearrange("a p t d -> (a p) t d"),
                             y_tile[r % 2][:, :, :]).then_inc(y_stored[r % 2], 16)

            def expert_step(q, r):
                weights, rows = ahead(3, q, r), ahead(4, q, r)
                if exists(weights[0]) and late(weights[0], 4):
                    load_weights(*weights)
                if exists(rows[0]):
                    load_rows(*rows)
                store_tile(*ahead(0, q, r))

            sp.wait_ge(experts_ready, 1)
            for k in range(4):
                load_weights(*ahead(k, 0, 0))
            sp.wait_ge(scattered, 16 * NT * TOPK)
            for k in range(4):
                load_rows(*ahead(k, 0, 0))
            experts(sp, expert_step)

            for g in range(NG):
                sp.wait_ge(row_added[TOPK - 1], GROUP * (g + 1))
                sp.wait_ge(acc_added, GROUP // 2 * (g + 1))
                cols = slice(g * GROUP * D, (g + 1) * GROUP * D)
                sp.dma_start(out[:, cols], acc[:, g * GROUP:(g + 1) * GROUP, :].rearrange("p j d -> p (j d)"))\
                    .then_inc(out_stored, 16)
            sp.wait_ge(out_stored, 16 * NG)

        @block.gpsimd
        def _(pool):
            pool.memset(zeros[:, :], 0.0).then_inc(zeros_set, 1)
            pool.memset(ident[:, :], 0.0).then_inc(zeros_set, 1)
            pool.memset(eps_tile[:, :], LN_EPS).then_inc(consts_set, 1)
            pool.memset(ones[:, :], 1.0).then_inc(consts_set, 1)
            pool.memset(head_of_row[:, :], 1.0).then_inc(zeros_set, 1)
            pool.memset(earlier[:, :], 1.0).then_inc(zeros_set, 1)
            pool.memset(scan_keep[:, :, :], 1.0).then_inc(zeros_set, 1)
            for i in range(2):
                pool.memset(v_aug[i][:, :, :, VC:AUG], 1.0).then_inc(consts_set, 1)
            pool.wait_ge(zeros_set, 5)
            pool.affine_select(out=ident[:, :], in_=ident[:, :], compare_op=ALU.not_equal, fill=1.0, base=0,
                               pattern=[[-1, P]], channel_multiplier=1).then_inc(ident_set, 1)
            pool.affine_select(out=head_of_row[:, :], in_=head_of_row[:, :], compare_op=ALU.is_ge, fill=0.0, base=0,
                               pattern=[[-HD, HEADS]], channel_multiplier=1).then_inc(zeros_set, 1)
            pool.affine_select(out=earlier[:, :], in_=earlier[:, :], compare_op=ALU.is_ge, fill=0.0, base=-1,
                               pattern=[[1, P]], channel_multiplier=-1).then_inc(consts_set, 1)
            pool.wait_ge(zeros_set, 6)
            pool.affine_select(out=head_of_row[:, :], in_=head_of_row[:, :], compare_op=ALU.is_ge, fill=0.0,
                               base=HD - 1, pattern=[[HD, HEADS]], channel_multiplier=-1).then_inc(ident_set, 1)
            pool.memset(scan_keep[:, :, 0:1], 0.0).then_inc(consts_set, 1)
            pool.iota(rank_of_expert[:, :], pattern=[[-1, E]], base=E, channel_multiplier=0,
                      allow_small_or_imprecise_dtypes=True).then_inc(consts_set, 1)
            pool.iota(tile_number[:, :, :], pattern=[[1, SLOT_TILES], [0, E]], base=0, channel_multiplier=0,
                      allow_small_or_imprecise_dtypes=True).then_inc(consts_set, 1)

            pool.wait_ge(weights_landed, 16 * N_WEIGHTS)
            for g in range(NG):
                tiles = acc[:, g * GROUP:(g + 1) * GROUP, :]
                pool.wait_ge(xn_by_dve, g + 1)
                pool.wait_ge(xn_by_act, g + 1)
                pool.tensor_tensor(tiles, tiles, xn[:, g * GROUP:(g + 1) * GROUP, :], ALU.add)\
                    .then_inc(base_added, 1)
                pool.wait_ge(base_added, 2 * g + 1)
                pool.tensor_tensor(tiles, tiles, over_tiles(b_out_sb, GROUP), ALU.add).then_inc(base_added, 1)

            pool.wait_ge(slots_ready, TOPK)
            pool.wait_ge(zeros_landed, 16 * (ST * SLOT_TILES // P // 2))
            for j in range(NT):
                i = routing_tile(j)
                for k in range(TOPK):
                    pool.indirect_dma_start(slots_x, bass.IndirectOffsetOnAxis(slot_i[k][:, i:i + 1], 0),
                                            xn[:, j, :], None).then_inc(scattered, 16)

            pool.wait_ge(y_stored[0], 16 * ((SLOT_TILES + 1) // 2))
            pool.wait_ge(y_stored[1], 16 * (SLOT_TILES // 2))
            for j in range(NT):
                i = routing_tile(j)
                if j >= RING:
                    pool.wait_ge(row_added[1], j - RING + 1)
                for k in range(TOPK):
                    pool.indirect_dma_start(y_back[:, j % RING, k, :], None, slots_y,
                                            bass.IndirectOffsetOnAxis(slot_i[k][:, i:i + 1], 0))\
                        .then_inc(gathered[j % RING], 16)
            for r in range(RING):
                pool.wait_ge(gathered[r], 16 * TOPK * (NT // RING))

        CONSTS = 8

        @block.tensor
        def _(pe):
            def feature_weights():
                pe.wait_ge(diag_ready, 1)
                diag = proj_diag[:, :, :].rearrange("p h f -> p (h f)")
                pe.matmul(bank[2][:, :], wkT_sb[:, :], diag, start=True, stop=True).then_inc(w_feat_ready, 1)
                pe.matmul(bank[3][:, :], wqT_sb[:, :], diag, start=True, stop=True).then_inc(w_feat_ready, 1)

            def keep_warm(n, free_bank):
                for _ in range(n):
                    pe.matmul(bank[free_bank][:, 0:P], ones[:, :], ones[:, :], start=True, stop=True)

            def transposes(g):
                if g >= 2:
                    pe.wait_ge(xnT_copied, g - 1)
                pe.wait_ge(xn_by_dve, g + 1)
                pe.wait_ge(xn_by_act, g + 1)
                for t in range(GROUP):
                    mm = pe.transpose(bank[g % 2][:, t * P:(t + 1) * P], xn[:, g * GROUP + t, :], ident[:, :])
                mm.then_inc(xnT_ready, 1)

            def router(g):
                pe.wait_ge(xnT_copied, g + 1)
                for t in range(GROUP):
                    j = g * GROUP + t
                    i = routing_tile(j)
                    mm = pe.matmul(bank[ROUTE_BANK][:, i * E:(i + 1) * E], xnT[:, j * P:(j + 1) * P],
                                   router_sb[:, :], start=True, stop=True)
                mm.then_inc(scores_ready, 1)

            pe.wait_ge(consts_set, CONSTS)
            keep_warm(24, 4)
            pe.wait_ge(ident_set, 1)
            pe.wait_ge(feature_weights_landed, 16 * N_FEATURE_WEIGHTS)
            for g in range(NG):
                transposes(g)
                if g >= 1:
                    router(g - 1)
                    keep_warm(1, 4)
                if g == 1:
                    feature_weights()

            def xT(f, par, half):
                if isinstance(f, int):
                    return xnT[:, (2 * f + half) * P:(2 * f + half + 1) * P]
                return xT_stage[par][:, half * P:(half + 1) * P]

            def z(n, f, f_half, par):
                if n == 0 and not isinstance(f, int):
                    pe.wait_ge(xT_staged[par], 16 * (f_half + par - ROUTED // 2))
                if late(f, 1):
                    pe.wait_ge(z_shifted, 4 * f + n - 3)
                pe.matmul(bank[Z_BANK + n][:, :], xT(f, par, n % 2), w_feat[:, n // 2, :],
                          start=True, stop=True).then_inc(z_ready, 1)

            def v(f, par):
                if late(f, 1):
                    pe.wait_ge(v_copied, f)
                for h in range(2):
                    mm = pe.matmul(bank[V_BANK][:, h * P:(h + 1) * P], xT(f, par, h),
                                   wv_sb[:, :], start=True, stop=True)
                mm.then_inc(v_ready, 1)

            def kv(b, par):
                pe.wait_ge(feat_ready, 4 * b + 2)
                pe.wait_ge(v_copied, b + 1)
                if late(b, 1):
                    pe.wait_ge(att_ready, b)
                if isinstance(b, int) and b == EARLY:
                    pe.wait_ge(y_copied, SLOT_TILES)
                for c in range(CH):
                    for h in range(2):
                        mm = pe.matmul(bank[KV_BANK][:, c * AUG:(c + 1) * AUG], feat[par][h][:, c * P:(c + 1) * P],
                                       v_aug[par][:, h, c, :], start=(h == 0), stop=(h == 1))
                mm.then_inc(kv_ready, 1)

            def qT(h, b, par):
                pe.wait_ge(feat_ready, 4 * b + 3 + h)
                if h == 1:
                    pe.wait_ge(qT_copied, 2 * b + 1)
                elif late(b, 2):
                    pe.wait_ge(acc_added, b - 1)
                for c in range(CH):
                    mm = pe.transpose(bank[QT_BANK][:, c * P:(c + 1) * P],
                                      feat[par][2 + h][:, c * P:(c + 1) * P], ident[:, :])
                mm.then_inc(qT_ready, 1)

            def numden(b, par):
                pe.wait_ge(qT_copied, 2 * b + 2)
                pe.wait_ge(kv_masked, b + 1)
                for h in range(2):
                    for c in range(CH):
                        at = ND + (h * CH + c) * AUG
                        mm = pe.matmul(bank[KV_BANK][:, at:at + AUG], qT_sb[h][:, c * P:(c + 1) * P],
                                       kv_sb[par][:, c, :], start=True, stop=True)
                mm.then_inc(nd_ready, 1)

            def attention_T(b):
                pe.wait_ge(att_ready, b + 1)
                for h in range(2):
                    mm = pe.transpose(bank[V_BANK][:, (2 + h) * P:(3 + h) * P], att[:, h * P:(h + 1) * P],
                                      ident[:, :])
                mm.then_inc(attT_ready, 1)

            def project(b, last):
                pe.wait_ge(attT_copied, b + 1)
                if not last:
                    pe.wait_ge(qT_copied, 2 * b + 4)
                for h in range(2):
                    mm = pe.matmul(bank[QT_BANK][:, h * P:(h + 1) * P], attT[:, h * P:(h + 1) * P],
                                   w_out_sb[:, :], start=True, stop=True)
                mm.then_inc(proj_ready, 1)

            def route_link(n):
                part = n % 5
                if n < 0:
                    router(NG - 1)
                elif n >= 5 * SINKHORN_ITERS:
                    if n == 5 * SINKHORN_ITERS + 1:
                        pe.wait_ge(mask_ready, 1)
                        pe.matmul(bank[ROUTE_BANK][:, 0:W], earlier[:, :], mask[:, :], start=True, stop=True)
                        pe.matmul(bank[ROUTE_BANK][:, W:2 * W], ones[:, :], mask[:, :], start=True, stop=True)\
                            .then_inc(counts_ready, 1)
                elif part == 2:
                    pe.wait_ge(row_normed, n // 5 + 1)
                    for h in range(2):
                        mm = pe.transpose(bank[ROUTE_BANK][:, h * P:(h + 1) * P], row_log[:, h * P:(h + 1) * P],
                                          ident[:, :])
                    mm.then_inc(cols_in, 1)
                elif part == 4:
                    pe.wait_ge(col_normed, n // 5 + 1)
                    for h in range(2):
                        mm = pe.transpose(bank[ROUTE_BANK][:, W + h * P:W + (h + 1) * P],
                                          col_log[:, h * P:(h + 1) * P], ident[:, :])
                    mm.then_inc(rows_in, 1)

            def step(b, b_half, par, front=True, back=True, tail=True, route=False):
                f, f_half, f_par = b + 1, b_half + par, 1 - par
                link = LINKS * f if route else None
                if front:
                    z(0, f, f_half, f_par)
                elif back:
                    keep_warm(6, ROUTE_BANK)
                if route:
                    route_link(link - 1)
                if front:
                    z(1, f, f_half, f_par)
                if route:
                    for n in range(3):
                        route_link(link + n)
                    z(2, f, f_half, f_par)
                if front:
                    v(f, f_par)
                if back:
                    kv(b, par)
                if tail:
                    attention_T(b - 1)
                if back:
                    qT(0, b, par)
                if route:
                    route_link(link + 3)
                    route_link(link + 4)
                    z(3, f, f_half, f_par)
                elif front:
                    z(2, f, f_half, f_par)
                if not front and back:
                    keep_warm(3, ROUTE_BANK)
                if back:
                    qT(1, b, par)
                if route:
                    route_link(link + 5)
                    route_link(link + 6)
                elif front:
                    z(3, f, f_half, f_par)
                if tail:
                    project(b - 1, last=not back)
                if not front and back:
                    keep_warm(3, ROUTE_BANK)
                if back:
                    numden(b, par)

            pe.wait_ge(xnT_copied, NG)
            pe.wait_ge(w_feat_copied, 2)
            attend_early(pe, step)

            def rows_T(k, q, r):
                pe.wait_ge(rows_landed[r % 2], 16 * (2 * q + r // 2 + 1))
                if late(k, 2):
                    pe.wait_ge(xT_copied, k - 1)
                for t in range(2):
                    mm = pe.transpose(bank[r % 2][:, t * P:(t + 1) * P], x_tile[r % 2][:, t, :], ident[:, :])
                mm.then_inc(xT_ready, 1)

            def up(k, q, r):
                pe.wait_ge(xT_copied, k + 1)
                pe.wait_ge(w_landed[r], 16 * (q + 1))
                if late(k, 2):
                    pe.wait_ge(hidden_ready, k - 1)
                for half in range(2):
                    for c in range(FC):
                        at = half * FF + c * P
                        mm = pe.matmul(bank[2 + 2 * half + r % 2][:, c * ST:(c + 1) * ST], w_tile[r][:, at:at + P],
                                       xT_tile[r % 2][:, :], start=True, stop=True)
                    mm.then_inc(up_ready, 1)

            def down(k, q, r):
                pe.wait_ge(hidden_ready, k + 1)
                if late(k, 2):
                    pe.wait_ge(y_copied, k - 1)
                for t in range(2):
                    for c in range(FC):
                        at = 2 * FF + c * D
                        mm = pe.matmul(bank[6 + r % 2][:, t * D:(t + 1) * D], hidden[r % 2][:, c, t * P:(t + 1) * P],
                                       w_tile[r][:, at:at + D], start=(c == 0), stop=(c == FC - 1))
                mm.then_inc(y_ready, 1)

            def expert_step(q, r):
                if exists(ahead(2, q, r)[0]):
                    rows_T(*ahead(2, q, r))
                if exists(ahead(1, q, r)[0]):
                    up(*ahead(1, q, r))
                down(*ahead(0, q, r))

            pe.wait_ge(v_copied, EARLY + 1)
            pe.wait_ge(z_shifted, 4 * (EARLY + 1))
            pe.wait_ge(acc_added, EARLY - 1)
            pe.wait_ge(att_ready, EARLY)
            rows_T(0, 0, 0)
            rows_T(1, 0, 1)
            up(0, 0, 0)
            experts(pe, expert_step)
            attend_late(step)

        @block.scalar
        def _(act):
            act.preload_act_table_set(SQRT_TABLE)
            for dst, src in ((router_sb[:, :], router_wT), (proj_sb[:, :], proj), (wkT_sb[:, :], wkT),
                             (wqT_sb[:, :], wqT)):
                act.dma_start(dst, src).then_inc(feature_weights_landed, 16)

            act.wait_ge(consts_set, CONSTS)

            def root(g):
                act.wait_ge(moments_done, g + 1)
                tiles = slice(g * GROUP, (g + 1) * GROUP)
                act.activation(std[:, tiles], moments[:, tiles, 1], ACT.Sqrt, bias=eps_tile[:, :])\
                    .then_inc(std_done, 1)

            def normalise(g):
                act.wait_ge(shift_done, g + 1)
                for j in range((g + 1) * GROUP - BY_ACT, (g + 1) * GROUP):
                    ins = act.activation(xn[:, j, :], acc[:, j, :], ACT.Identity, bias=shift[:, j:j + 1],
                                         scale=rstd[:, j:j + 1])
                ins.then_inc(xn_by_act, 1)

            def copy_xnT(g):
                act.wait_ge(xnT_ready, g + 1)
                act.copy(xnT[:, g * GROUP * P:(g + 1) * GROUP * P], bank[g % 2][:, :]).then_inc(xnT_copied, 1)

            for g in range(NG + 2):
                if g < NG:
                    root(g)
                if 1 <= g <= NG:
                    normalise(g - 1)
                if g >= 2:
                    copy_xnT(g - 2)
                if g == 3:
                    for n in range(2):
                        act.wait_ge(w_feat_ready, n + 1)
                        act.copy(w_feat[:, n, :], bank[2 + n][:, :]).then_inc(w_feat_copied, 1)
            act.preload_act_table_set(EXP_LN_TABLE)

            def features(n, f, par):
                act.wait_ge(z_shifted, 4 * f + n + 1)
                if late(f, 2):
                    if n < 2:
                        act.wait_ge(kv_ready, f - 1)
                    else:
                        act.wait_ge(qT_ready, 2 * f - 4 + n - 1)
                act.activation(feat[par][n][:, :], z_sb[n][:, :], ACT.Exp).then_inc(feat_ready, 1)

            def copy_v(f, par):
                act.wait_ge(v_ready, f + 1)
                if late(f, 2):
                    act.wait_ge(kv_ready, f - 1)
                act.copy(v_aug[par][:, :, :, 0:VC], bank[V_BANK][:, 0:2 * P]
                         .rearrange("p (h c v) -> p h c v", h=2, c=CH)).then_inc(v_copied, 1)

            def copy_qT(h, b):
                act.wait_ge(qT_ready, 2 * b + h + 1)
                if late(b, 1):
                    act.wait_ge(nd_ready, b)
                act.copy(qT_sb[h][:, :], bank[QT_BANK][:, :]).then_inc(qT_copied, 1)

            def copy_attT(b):
                act.wait_ge(attT_ready, b + 1)
                if late(b, 1):
                    act.wait_ge(proj_ready, b)
                act.copy(attT[:, :], bank[V_BANK][:, 2 * P:4 * P]).then_inc(attT_copied, 1)

            def route_link(n):
                it, part = n // 5, n % 5
                if n == 5 * SINKHORN_ITERS:
                    act.wait_ge(rows_in, SINKHORN_ITERS)
                    act.activation(gate_exp[:, :], bank[ROUTE_BANK][:, W:2 * W], ACT.Exp).then_inc(gates_exped, 1)
                elif n < 5 * SINKHORN_ITERS:
                    if part == 0:
                        act.wait_ge(row_shifted, it + 1)
                        act.activation(row_exp[:, :], row_shift[:, :], ACT.Exp).then_inc(row_exped, 1)
                    elif part == 1:
                        act.wait_ge(row_summed, it + 1)
                        act.activation(row_ln[:, :], row_sum[:, :], ACT.Ln).then_inc(row_lned, 1)
                    elif part == 3:
                        act.wait_ge(col_maxed, it + 1)
                        act.activation(col_exp[:, :], bank[ROUTE_BANK][:, 0:W], ACT.Exp, bias=col_negmax[:, :],
                                       accum_out=col_sum[:, :]).then_inc(col_summed, 1)
                        act.wait_ge(col_summed, it + 1)
                        act.activation(col_ln[:, :], col_sum[:, :], ACT.Ln).then_inc(col_lned, 1)

            def step(b, b_half, par, front=True, back=True, tail=True, route=False):
                f, f_par = b + 1, 1 - par
                link = LINKS * f if route else None
                def links(*slots):
                    for n in slots:
                        if route:
                            route_link(link + n)

                links(0)
                if front:
                    features(0, f, f_par)
                links(1, 2)
                if front:
                    features(1, f, f_par)
                links(3, 4)
                if tail:
                    copy_attT(b - 1)
                if front:
                    copy_v(f, f_par)
                if back:
                    copy_qT(0, b)
                if route:
                    features(2, f, f_par)
                    links(5, 6)
                if back:
                    copy_qT(1, b)
                if front and not route:
                    features(2, f, f_par)
                if front:
                    features(3, f, f_par)
                links(7)

            attend_early(act, step)

            def copy_xT(k, q, r):
                act.wait_ge(xT_ready, k + 1)
                if late(k, 2):
                    act.wait_ge(up_ready, 2 * k - 2)
                act.copy(xT_tile[r % 2][:, :], bank[r % 2][:, 0:ST]).then_inc(xT_copied, 1)

            def relu(k, q, r):
                act.wait_ge(up_ready, 2 * k + 1)
                if late(k, 2):
                    act.wait_ge(hidden_ready, k - 1)
                act.activation(gate_act[r % 2][:, :], bank[2 + r % 2][:, :], ACT.Relu).then_inc(relu_done, 1)

            def expert_step(q, r):
                if exists(ahead(2, q, r)[0]):
                    copy_xT(*ahead(2, q, r))
                if exists(ahead(1, q, r)[0]):
                    relu(*ahead(1, q, r))

            copy_xT(0, 0, 0)
            copy_xT(1, 0, 1)
            relu(0, 0, 0)
            experts(act, expert_step)
            attend_late(step)

        @block.vector
        def _(dve):
            dve.memset(chunk_mask[:, :], 0.0).then_inc(chunk_mask_set, 1)
            dve.wait_ge(chunk_mask_set, 1)
            for m in range(HC):
                rows = slice(F * m, F * (m + 1))
                dve.memset(chunk_mask[rows, HD * m:HD * (m + 1)], 1.0).then_inc(chunk_mask_set, 1)
                dve.memset(chunk_mask[rows, VC + m:VC + m + 1], 1.0).then_inc(chunk_mask_set, 1)

            def statistics(g):
                dve.wait_ge(x_landed[g], 16)
                for t in range(GROUP):
                    ins = dve.bn_stats(stats[:, g * GROUP + t, :], acc[:, g * GROUP + t, :])
                ins.then_inc(stats_done, 1)
                dve.wait_ge(stats_done, g + 1)
                for t in range(GROUP):
                    ins = dve.bn_aggr(moments[:, g * GROUP + t, :], stats[:, g * GROUP + t, :])
                ins.then_inc(moments_done, 1)

            def normalise(g):
                tiles = slice(g * GROUP, (g + 1) * GROUP)
                dve.wait_ge(std_done, g + 1)
                dve.reciprocal(rstd[:, tiles], std[:, tiles]).then_inc(rstd_done, 1)
                dve.wait_ge(rstd_done, g + 1)
                dve.scalar_tensor_tensor(shift[:, tiles], moments[:, tiles, 0], -1.0, rstd[:, tiles],
                                         ALU.mult, ALU.mult).then_inc(shift_done, 1)
                for t in range(GROUP - BY_ACT):
                    j = g * GROUP + t
                    ins = dve.tensor_scalar(xn[:, j, :], acc[:, j, :], moments[:, j, 0:1], rstd[:, j:j + 1],
                                            ALU.subtract, ALU.mult)
                ins.then_inc(xn_by_dve, 1)

            for g in range(NG + 1):
                if g < NG:
                    statistics(g)
                if g >= 1:
                    normalise(g - 1)
                if g == 1:
                    dve.wait_ge(feature_weights_landed, 16 * N_FEATURE_WEIGHTS)
                    dve.wait_ge(ident_set, 2)
                    dve.tensor_tensor(proj_diag[:, :, :], over_tiles(proj_sb, HEADS), wide(head_of_row, F), ALU.mult)\
                        .then_inc(diag_ready, 1)

            def z(n, f, link=None):
                args = bank[Z_BANK + n][:, :].rearrange("p (h f) -> p h f", f=F)
                dve.wait_ge(z_ready, 4 * f + n + 1)
                dve.tensor_reduce(neg_max[n][:, :], args, AX_X, ALU.max, negate=True).then_inc(z_negmax, 1)
                if link is not None:
                    route_link(link + 2 * n)
                dve.wait_ge(z_negmax, 4 * f + n + 1)
                if late(f, 1):
                    dve.wait_ge(feat_ready, 4 * f + n - 3)
                dve.tensor_tensor(z_sb[n][:, :].rearrange("p (h f) -> p h f", f=F), args, wide(neg_max[n], F), ALU.add)\
                    .then_inc(z_shifted, 1)
                if link is not None:
                    route_link(link + 2 * n + 1)

            def mask_kv(b, par):
                dve.wait_ge(kv_ready, b + 1)
                if late(b, 2):
                    dve.wait_ge(nd_ready, b - 1)
                dve.tensor_tensor(kv_sb[par][:, :, :], bank[KV_BANK][:, 0:CH * AUG].rearrange("p (c a) -> p c a", c=CH),
                                  over_tiles(chunk_mask, CH), ALU.mult).then_inc(kv_masked, 1)

            def divide(b):
                nd = bank[KV_BANK][:, ND:ND + 2 * CH * AUG].rearrange("p (c a) -> p c a", a=AUG)
                dve.wait_ge(nd_ready, b + 1)
                dve.tensor_scalar(den[:, :, :], nd[:, :, VC:AUG], DEN_EPS, None, ALU.add).then_inc(den_step, 1)
                dve.wait_ge(den_step, 2 * b + 1)
                dve.reciprocal(inv_den[:, :, :], den[:, :, :]).then_inc(den_step, 1)
                dve.wait_ge(den_step, 2 * b + 2)
                if late(b, 1):
                    dve.wait_ge(attT_ready, b)
                dve.tensor_tensor(att[:, :].rearrange("p (c m d) -> p c m d", c=2 * CH, m=HC),
                                  nd[:, :, 0:VC].rearrange("p c (m d) -> p c m d", m=HC),
                                  inv_den[:, :, :].unsqueeze(3).broadcast_to([P, 2 * CH, HC, HD]), ALU.mult)\
                    .then_inc(att_ready, 1)

            def add_projection(b):
                dve.wait_ge(proj_ready, b + 1)
                if not late(b, 1):
                    dve.wait_ge(base_added, 2 * NG)
                tiles = acc[:, bass.ds(2 * b, 2), :]
                dve.tensor_tensor(tiles, bank[QT_BANK][:, 0:2 * P].rearrange("p (t d) -> p t d", t=2), tiles, ALU.add)\
                    .then_inc(acc_added, 1)

            def combine(g, k):
                if k == 0:
                    dve.wait_ge(acc_added, min((g + 1) * GROUP // 2, EARLY + g))
                for j in range(g * GROUP, (g + 1) * GROUP):
                    if k == 0:
                        dve.wait_ge(gathered[j % RING], 16 * TOPK * (j // RING + 1))
                    else:
                        dve.wait_ge(row_added[0], j + 1)
                    i = routing_tile(j)
                    dve.scalar_tensor_tensor(acc[:, j, :], y_back[:, j % RING, k, :], weight[k][:, i:i + 1],
                                             acc[:, j, :], ALU.mult, ALU.add).then_inc(row_added[k], 1)

            own = [0]

            def settle(ins):
                own[0] += 1
                ins.then_inc(route_step, 1)
                dve.wait_ge(route_step, own[0])

            def choose(k, values):
                settle(dve.tensor_reduce(top[k][:, :], by_tile(values), AX_X, ALU.max))
                settle(dve.tensor_tensor(by_tile(is_best), by_tile(values), wide(top[k], E), ALU.is_equal))
                settle(dve.tensor_tensor(by_tile(ranked), by_tile(is_best), over_tiles(rank_of_expert, NT), ALU.mult))
                settle(dve.tensor_reduce(best_rank[:, :], by_tile(ranked), AX_X, ALU.max))
                settle(dve.tensor_tensor(by_tile(chosen[k]), by_tile(ranked), wide(best_rank, E), ALU.is_equal))

            def route_link(n):
                it, part = n // 5, n % 5
                if n < 5 * SINKHORN_ITERS:
                    if part == 0:
                        if it == 0:
                            dve.wait_ge(scores_ready, NG)
                            settle(dve.tensor_tensor(
                                by_tile(scores), bank[ROUTE_BANK][:, 0:W].rearrange("p (i e) -> p i e", e=E),
                                over_tiles(router_b_sb, NT), ALU.add))
                            settle(dve.tensor_scalar(scores[:, :], scores[:, :], inv_temp[:, :], None, ALU.mult))
                            src = scores[:, :]
                        else:
                            dve.wait_ge(rows_in, it)
                            src = bank[ROUTE_BANK][:, W:2 * W]
                        src = src.rearrange("p (i e) -> p i e", e=E)
                        settle(dve.tensor_reduce(row_max[:, :], src, AX_X, ALU.max))
                        dve.tensor_tensor(by_tile(row_shift), src, wide(row_max, E), ALU.subtract)\
                            .then_inc(row_shifted, 1)
                    elif part == 1:
                        dve.wait_ge(row_exped, it + 1)
                        dve.tensor_reduce(row_sum[:, :], by_tile(row_exp), AX_X, ALU.add).then_inc(row_summed, 1)
                    elif part == 2:
                        dve.wait_ge(row_lned, it + 1)
                        dve.tensor_tensor(by_tile(row_log), by_tile(row_shift), wide(row_ln, E), ALU.subtract)\
                            .then_inc(row_normed, 1)
                    elif part == 3:
                        dve.wait_ge(cols_in, it + 1)
                        dve.tensor_reduce(col_negmax[:, :], bank[ROUTE_BANK][:, 0:W], AX_X, ALU.max, negate=True)\
                            .then_inc(col_maxed, 1)
                    elif part == 4:
                        dve.wait_ge(col_lned, it + 1)
                        dve.tensor_scalar(col_log[:, :], bank[ROUTE_BANK][:, 0:W], col_negmax[:, :], col_ln[:, :],
                                          ALU.add, ALU.subtract).then_inc(col_normed, 1)
                elif n == 5 * SINKHORN_ITERS:
                    dve.wait_ge(gates_exped, 1)
                    settle(dve.tensor_reduce(gate_sum[:, :], by_tile(gate_exp), AX_X, ALU.add))
                    settle(dve.tensor_scalar(gate_sum[:, :], gate_sum[:, :], GATE_EPS, None, ALU.add))
                    settle(dve.reciprocal(gate_inv[:, :], gate_sum[:, :]))
                    settle(dve.tensor_tensor(by_tile(gates), by_tile(gate_exp), wide(gate_inv, E), ALU.mult))
                    choose(0, gates)
                elif n == 5 * SINKHORN_ITERS + 1:
                    settle(dve.scalar_tensor_tensor(rest[:, :], chosen[0][:, :], -4.0, gates[:, :], ALU.mult, ALU.add))
                    choose(1, rest)
                    dve.tensor_tensor(mask[:, :], chosen[0][:, :], chosen[1][:, :], ALU.add).then_inc(mask_ready, 1)
                elif n == 5 * SINKHORN_ITERS + 2:
                    place()
                elif n == 5 * SINKHORN_ITERS + 3:
                    settle(dve.tensor_tensor(top_sum[:, :], top[0][:, :], top[1][:, :], ALU.add))
                    settle(dve.tensor_scalar(top_sum[:, :], top_sum[:, :], GATE_EPS, None, ALU.add))
                    settle(dve.reciprocal(top_inv[:, :], top_sum[:, :]))
                    for k in range(TOPK):
                        settle(dve.tensor_tensor(weight[k][:, :], top[k][:, :], top_inv[:, :], ALU.mult))

            def place():
                dve.wait_ge(counts_ready, 1)
                settle(dve.tensor_copy(totals[:, :, :].rearrange("p e i -> p i e"),
                                       bank[ROUTE_BANK][:, W:2 * W].rearrange("p (i e) -> p i e", e=E)))
                settle(dve.tensor_tensor_scan(prefix[:, :, :].rearrange("p e i -> p (e i)"),
                                              scan_keep[:, :, :].rearrange("p e i -> p (e i)"),
                                              totals[:, :, :].rearrange("p e i -> p (e i)"), 0.0, ALU.mult, ALU.add))
                settle(dve.tensor_scalar(padded_i[:, :], prefix[:, :, NT - 1], float(ST - 1), None, ALU.add))
                settle(dve.tensor_scalar(tiles_i[:, :], padded_i[:, :], ST.bit_length() - 1, None,
                                         ALU.logical_shift_right))
                settle(dve.tensor_copy(tiles_f[:, :], tiles_i[:, :]))
                settle(dve.tensor_tensor_scan(tiles_end[:, :], ones[:, 0:E], tiles_f[:, :], 0.0, ALU.mult, ALU.add))
                settle(dve.tensor_tensor(first_slot[:, :], tiles_end[:, :], tiles_f[:, :], ALU.subtract))
                settle(dve.tensor_scalar(first_slot[:, :], first_slot[:, :], float(ST), None, ALU.mult))
                settle(dve.tensor_tensor(start[:, :, :], prefix[:, :, :], totals[:, :, :], ALU.subtract))
                settle(dve.tensor_tensor(start[:, :, :], start[:, :, :], wide(first_slot, NT), ALU.add))
                settle(dve.tensor_tensor(by_tile(position), bank[ROUTE_BANK][:, 0:W].rearrange("p (i e) -> p i e", e=E),
                                         start[:, :, :].rearrange("p e i -> p i e"), ALU.add))
                for k in range(TOPK):
                    settle(dve.tensor_tensor(picked[k][:, :], chosen[k][:, :], position[:, :], ALU.mult))
                    settle(dve.tensor_reduce(slot_f[k][:, :], by_tile(picked[k]), AX_X, ALU.add))
                    dve.tensor_copy(slot_i[k][:, :], slot_f[k][:, :]).then_inc(slots_ready, 1)
                settle(dve.tensor_tensor(past[:, :, :], tile_number[:, :, :], over_tiles(tiles_end, SLOT_TILES), ALU.is_ge))
                settle(dve.tensor_reduce(expert_f[:, :], past[:, :, :], AX_X, ALU.add))
                dve.tensor_scalar(expert_i[:, :], expert_f[:, :], float(E - 1), None, ALU.min).then_inc(experts_ready, 1)

            def step(b, b_half, par, front=True, back=True, tail=True, route=False, group=None):
                f = b + 1
                link = LINKS * f if route else None
                if tail and not (isinstance(b, int) and b == EARLY):
                    divide(b - 1)
                if front:
                    z(0, f, link)
                    z(1, f, link)
                if back:
                    mask_kv(b, par)
                if group is not None:
                    combine(group, 0)
                if front:
                    z(2, f, link)
                if group is not None:
                    combine(group, 1)
                if front:
                    z(3, f, link)
                if tail:
                    if group is not None:
                        dve.wait_ge(row_added[TOPK - 1], (group + 1) * GROUP)
                    add_projection(b - 1)

            dve.wait_ge(chunk_mask_set, 1 + 2 * HC)
            dve.wait_ge(consts_set, CONSTS)
            dve.wait_ge(weights_landed, 16 * N_WEIGHTS)
            settle(dve.tensor_scalar(temp_lim[:, :], temp_sb[:, :], 0.1, None, ALU.max))
            settle(dve.reciprocal(inv_temp[:, :], temp_lim[:, :]))
            attend_early(dve, step)
            divide(EARLY - 1)

            def multiply(k, q, r):
                dve.wait_ge(relu_done, k + 1)
                dve.wait_ge(up_ready, 2 * k + 2)
                if late(k, 2):
                    dve.wait_ge(y_ready, k - 1)
                dve.tensor_tensor(hidden[r % 2][:, :, :].rearrange("p c s -> p (c s)"), bank[4 + r % 2][:, :],
                                  gate_act[r % 2][:, :], ALU.mult).then_inc(hidden_ready, 1)

            def copy_y(k, q, r):
                dve.wait_ge(y_ready, k + 1)
                if late(k, 2):
                    dve.wait_ge(y_stored[r % 2], 16 * (2 * q + r // 2))
                dve.tensor_copy(y_tile[r % 2][:, :, :].rearrange("p t d -> p (t d)"), bank[6 + r % 2][:, 0:2 * D])\
                    .then_inc(y_copied, 1)

            def expert_step(q, r):
                if exists(ahead(1, q, r)[0]):
                    multiply(*ahead(1, q, r))
                copy_y(*ahead(0, q, r))

            multiply(0, 0, 0)
            experts(dve, expert_step)

            def late_step(b, b_half, par, front, back):
                group = b - EARLY - 1 if EARLY < b <= EARLY + NG else None
                step(b, b_half, par, front=front, back=back, group=group)

            attend_late(late_step)
            for g in range(NB - EARLY, NG):
                combine(g, 0)
                combine(g, 1)


def kernel(L0_attn_x, L0_attn_w_qkv, L0_attn_w_out, L0_attn_b_out, L0_attn_proj, L0_ffn_router_w, L0_ffn_router_b,
           L0_ffn_temperature, L0_ffn_wg, L0_ffn_wp, L0_ffn_wo):
    import numpy as np
    import concourse.bacc as bacc
    from concourse.bass_utils import run_bass_kernel_spmd

    x = np.asarray(L0_attn_x)
    B, T, D = x.shape
    NT = B * T // P
    w_qkv = np.asarray(L0_attn_w_qkv)
    wg, wp, wo = (np.asarray(a) for a in (L0_ffn_wg, L0_ffn_wp, L0_ffn_wo))
    E, _, FF = wg.shape
    wo_rows = wo.reshape(E, FF // P, P, D).transpose(0, 2, 1, 3).reshape(E, P, FF // P * D)
    arrays = {
        "x_dram": x.reshape(NT, P, D).transpose(1, 0, 2).reshape(P, NT * D),
        "wqT_dram": w_qkv[:, 0:D].T,
        "wkT_dram": w_qkv[:, D:2 * D].T,
        "wv_dram": w_qkv[:, 2 * D:3 * D],
        "w_out_dram": np.asarray(L0_attn_w_out),
        "b_out_dram": np.asarray(L0_attn_b_out).reshape(1, D),
        "proj_dram": np.asarray(L0_attn_proj).reshape(D, -1),
        "router_wT_dram": np.asarray(L0_ffn_router_w).T,
        "router_b_dram": np.asarray(L0_ffn_router_b).reshape(1, E),
        "temperature_dram": np.asarray(L0_ffn_temperature).reshape(1, 1),
        "w_expert_dram": np.concatenate([wg, wp, wo_rows], axis=2),
    }
    arrays = {n: np.ascontiguousarray(a) for n, a in arrays.items()}
    nc = bacc.Bacc("TRN2", target_bir_lowering=False, num_devices=1)
    args = [nc.dram_tensor(n, a.shape, mybir.dt.from_np(a.dtype), kind="ExternalInput").ap() for n, a in arrays.items()]
    out = nc.dram_tensor("out_dram", (P, NT * D), F32, kind="ExternalOutput").ap()
    build_program(nc, *args, out)
    r = run_bass_kernel_spmd(nc, [arrays], core_ids=[0])
    got = np.asarray(r.results[0]["out_dram"])
    return got.reshape(P, NT, D).transpose(1, 0, 2).reshape(B, T, D)
```

```python
from contextlib import ExitStack

import concourse.bass as bass
from concourse import mybir

F32 = mybir.dt.float32
F32R = mybir.dt.float32r
I32 = mybir.dt.int32
ALU = mybir.AluOpType
ACT = mybir.ActivationFunctionType
AX_X = mybir.AxisListType.X

P = 128
LN_EPS = 1e-5
DEN_EPS = 1e-6
GATE_EPS = 1e-8
SINKHORN_ITERS = 3
SQRT_TABLE = "sqrt_and_others"
EXP_LN_TABLE = "natural_log_exp_and_others"


def build_program(nc, x, wqT, wkT, wv, w_out, b_out, proj, router_wT, router_b, temperature, w_expert, out):
    D = wv.shape[0]
    NT = x.shape[1] // D
    NB = NT // 2
    HEADS, F = 16, proj.shape[1]
    HD = D // HEADS
    E = router_wT.shape[1]
    FF = w_expert.shape[2] // 3
    FC = FF // P
    FEAT = HEADS * F
    CH = FEAT // P
    HC = HEADS // CH
    VC = HC * HD
    AUG = VC + HC
    TOPK = 2
    ST = 256
    SLOT_TILES = (NT * P * TOPK - E) // ST + E
    LOOP = 6
    GROUP = 4
    NG = NT // GROUP
    RING = 8
    BY_ACT = 2
    LOOP_FROM = 2
    LINKS = 8
    LAST_LINKS = 3
    EARLY = 8

    slots_x = nc.dram_tensor("slots_x", [SLOT_TILES * ST, D], F32, kind="Internal").ap()
    slots_y = nc.dram_tensor("slots_y", [SLOT_TILES * ST, D], F32, kind="Internal").ap()

    with ExitStack() as ctx:
        def sb(name, shape, dt=F32):
            return ctx.enter_context(nc.sbuf_tensor(name, shape, dt))

        def sem(name):
            return ctx.enter_context(nc.semaphore(name))

        ident = sb("ident", [P, P])
        ones = sb("ones", [P, P])
        earlier = sb("earlier", [P, P])
        head_of_row = sb("head_of_row", [P, HEADS])
        chunk_mask = sb("chunk_mask", [P, AUG])
        rank_of_expert = sb("rank_of_expert", [P, E])
        tile_number = sb("tile_number", [P, SLOT_TILES, E])
        scan_keep = sb("scan_keep", [P, E, NT])
        eps_tile = sb("eps_tile", [P, 1])
        zeros = sb("zeros", [P, 2 * D])

        acc = sb("acc", [P, NT, D])
        xn = sb("xn", [P, NT, D])
        xnT = sb("xnT", [P, NT * P])
        wqT_sb, wkT_sb, wv_sb, w_out_sb = (sb(n, [P, D]) for n in ("wqT_sb", "wkT_sb", "wv_sb", "w_out_sb"))
        b_out_sb = sb("b_out_sb", [P, D])
        proj_sb = sb("proj_sb", [P, F])
        proj_diag = sb("proj_diag", [P, HEADS, F])
        w_feat = sb("w_feat", [P, 2, FEAT])
        router_sb = sb("router_sb", [P, E])
        router_b_sb = sb("router_b_sb", [P, E])
        temp_sb = sb("temp_sb", [P, 1])
        temp_lim = sb("temp_lim", [P, 1])
        inv_temp = sb("inv_temp", [P, 1])
        stats = sb("stats", [P, NT, 6])
        moments = sb("moments", [P, NT, 2])
        std = sb("std", [P, NT])
        rstd = sb("rstd", [P, NT])
        shift = sb("shift", [P, NT])

        xT_stage = [sb(f"xT_stage{i}", [P, 2 * P]) for i in range(2)]
        v_aug = [sb(f"v_aug{i}", [P, 2, CH, AUG]) for i in range(2)]
        neg_max = [sb(f"neg_max{n}", [P, HEADS]) for n in range(4)]
        z_sb = [sb(f"z_sb{n}", [P, FEAT]) for n in range(4)]
        feat = [[sb(f"feat{i}_{n}", [P, FEAT]) for n in range(4)] for i in range(2)]
        kv_sb = [sb(f"kv_sb{i}", [P, CH, AUG]) for i in range(2)]
        qT_sb = [sb(f"qT_sb{h}", [P, CH * P]) for h in range(2)]
        den = sb("den", [P, 2 * CH, HC])
        inv_den = sb("inv_den", [P, 2 * CH, HC])
        att = sb("att", [P, 2 * P])
        attT = sb("attT", [P, 2 * P])

        W = NT * E
        scores = sb("scores", [P, W])
        row_max, row_sum, row_ln = (sb(n, [P, NT]) for n in ("row_max", "row_sum", "row_ln"))
        row_shift, row_exp, row_log = (sb(n, [P, W]) for n in ("row_shift", "row_exp", "row_log"))
        col_negmax, col_sum, col_ln = (sb(n, [P, 1]) for n in ("col_negmax", "col_sum", "col_ln"))
        col_exp, col_log = (sb(n, [P, 2 * P]) for n in ("col_exp", "col_log"))
        gate_exp, gates, rest = (sb(n, [P, W]) for n in ("gate_exp", "gates", "rest"))
        gate_sum, gate_inv, best_rank = (sb(n, [P, NT]) for n in ("gate_sum", "gate_inv", "best_rank"))
        top = [sb(f"top{k}", [P, NT]) for k in range(TOPK)]
        chosen = [sb(f"chosen{k}", [P, W]) for k in range(TOPK)]
        is_best, ranked, mask = (sb(n, [P, W]) for n in ("is_best", "ranked", "mask"))
        top_sum, top_inv = sb("top_sum", [P, NT]), sb("top_inv", [P, NT])
        weight = [sb(f"weight{k}", [P, NT]) for k in range(TOPK)]
        totals, prefix, start = (sb(n, [P, E, NT]) for n in ("totals", "prefix", "start"))
        position, picked = sb("position", [P, W]), [sb(f"picked{k}", [P, W]) for k in range(TOPK)]
        padded_i, tiles_i = sb("padded_i", [P, E], I32), sb("tiles_i", [P, E], I32)
        tiles_f, tiles_end, first_slot = (sb(n, [P, E]) for n in ("tiles_f", "tiles_end", "first_slot"))
        slot_f = [sb(f"slot_f{k}", [P, NT]) for k in range(TOPK)]
        slot_i = [sb(f"slot_i{k}", [P, NT], I32) for k in range(TOPK)]
        past = sb("past", [P, SLOT_TILES, E])
        expert_f = sb("expert_f", [P, SLOT_TILES])
        expert_i = sb("expert_i", [P, SLOT_TILES], I32)

        w_tile = [sb(f"w_tile{i}", [P, 3 * FF]) for i in range(LOOP)]
        x_tile = [sb(f"x_tile{i}", [P, 2, D]) for i in range(2)]
        w_high = [sb(f"w_high{i}", [P, 2 * FF], F32R) for i in range(2)]
        w_low = [sb(f"w_low{i}", [P, 2 * FF], F32R) for i in range(2)]
        xT_high = [sb(f"xT_high{i}", [P, ST], F32R) for i in range(2)]
        xT_low = [sb(f"xT_low{i}", [P, ST], F32R) for i in range(2)]
        gate_act = [sb(f"gate_act{i}", [P, FC * ST]) for i in range(2)]
        hidden = [sb(f"hidden{i}", [P, FC, ST]) for i in range(2)]
        y_tile = [sb(f"y_tile{i}", [P, 2, D]) for i in range(2)]
        y_back = sb("y_back", [P, RING, TOPK, D])

        bank = [ctx.enter_context(nc.psum_tensor(f"bank{i}", [P, 512], F32)) for i in range(8)]
        V_BANK, Z_BANK, QT_BANK, KV_BANK, ROUTE_BANK = 0, 1, 5, 6, 7
        ND = CH * AUG

        x_landed = [sem(f"x_landed{g}") for g in range(NG)]
        feature_weights_landed, weights_landed, zeros_landed = (
            sem(n) for n in ("feature_weights_landed", "weights_landed", "zeros_landed"))
        zeros_set, consts_set, ident_set, chunk_mask_set = (
            sem(n) for n in ("zeros_set", "consts_set", "ident_set", "chunk_mask_set"))
        stats_done, moments_done, std_done, rstd_done, shift_done = (
            sem(n) for n in ("stats_done", "moments_done", "std_done", "rstd_done", "shift_done"))
        xn_by_dve, xn_by_act = sem("xn_by_dve"), sem("xn_by_act")
        xnT_ready, xnT_copied, scores_ready, base_added = (
            sem(n) for n in ("xnT_ready", "xnT_copied", "scores_ready", "base_added"))
        diag_ready, w_feat_ready, w_feat_copied = sem("diag_ready"), sem("w_feat_ready"), sem("w_feat_copied")
        xT_staged = [sem(f"xT_staged{i}") for i in range(2)]
        z_ready, z_negmax, z_shifted, feat_ready = (
            sem(n) for n in ("z_ready", "z_negmax", "z_shifted", "feat_ready"))
        v_ready, v_copied, kv_ready, kv_masked = (sem(n) for n in ("v_ready", "v_copied", "kv_ready", "kv_masked"))
        qT_ready, qT_copied, nd_ready, den_step, att_ready = (
            sem(n) for n in ("qT_ready", "qT_copied", "nd_ready", "den_step", "att_ready"))
        attT_ready, attT_copied, proj_ready, acc_added = (
            sem(n) for n in ("attT_ready", "attT_copied", "proj_ready", "acc_added"))
        route_step = sem("route_step")
        row_shifted, row_exped, row_summed, row_lned, row_normed = (
            sem(n) for n in ("row_shifted", "row_exped", "row_summed", "row_lned", "row_normed"))
        cols_in, col_maxed, col_summed, col_lned, col_normed, rows_in = (
            sem(n) for n in ("cols_in", "col_maxed", "col_summed", "col_lned", "col_normed", "rows_in"))
        gates_exped, mask_ready, counts_ready, slots_ready, experts_ready = (
            sem(n) for n in ("gates_exped", "mask_ready", "counts_ready", "slots_ready", "experts_ready"))
        scattered = sem("scattered")
        w_landed = [sem(f"w_landed{i}") for i in range(LOOP)]
        rows_landed = [sem(f"rows_landed{i}") for i in range(2)]
        y_stored = [sem(f"y_stored{i}") for i in range(2)]
        w_high_ready, w_low_ready, xT_high_ready, xT_low_ready = (
            sem(n) for n in ("w_high_ready", "w_low_ready", "xT_high_ready", "xT_low_ready"))
        xT_ready, up_ready, relu_done, hidden_ready, y_ready, y_copied = (
            sem(n) for n in ("xT_ready", "up_ready", "relu_done", "hidden_ready", "y_ready", "y_copied"))
        gathered = [sem(f"gathered{i}") for i in range(RING)]
        row_added = [sem(f"row{k}_added") for k in range(TOPK)]
        out_stored = sem("out_stored")

        N_FEATURE_WEIGHTS, N_WEIGHTS = 4, 5

        def routing_tile(j):
            return (j % 2) * NB + j // 2

        def by_tile(t):
            return t[:, :].rearrange("p (i e) -> p i e", e=E)

        def wide(t, n):
            return t[:, :].unsqueeze(2).broadcast_to([P, t.shape[1], n])

        def over_tiles(t, n):
            return t[:, :].unsqueeze(1).broadcast_to([P, n, t.shape[1]])

        def qT_bank(h, route):
            return QT_BANK if h == 0 or route else ROUTE_BANK

        def late(v, n):
            return not isinstance(v, int) or v >= n

        def attend_early(engine, step):
            step(-1, -1, 1, back=False, tail=False, route=True)
            step(0, 0, 0, tail=False, route=True)
            for b in range(1, LOOP_FROM):
                step(b, b // 2, b % 2)
            with engine.Fori(LOOP_FROM // 2, EARLY // 2) as i:
                step(2 * i, i, 0)
                step(2 * i + 1, i, 1)

        def attend_late(step):
            for b in range(EARLY, NB + 1):
                step(b, b // 2, b % 2, front=b + 1 < NB, back=b < NB)

        def ahead(n, q, r):
            return LOOP * q + r + n, q + (r + n) // LOOP, (r + n) % LOOP

        def before(q, r):
            return LOOP // 2 * q + r // 2

        def exists(k):
            return not isinstance(k, int) or k < SLOT_TILES

        def experts(engine, step):
            for k in range(LOOP):
                step(k // LOOP, k % LOOP)
            last = (SLOT_TILES - LOOP + 1) // LOOP
            with engine.Fori(1, last) as q:
                for r in range(LOOP):
                    step(q, r)
            for k in range(LOOP * last, SLOT_TILES):
                step(k // LOOP, k % LOOP)

        block = ctx.enter_context(nc.Block())

        @block.sync
        def _(sp):
            for g in range(NG):
                cols = slice(g * GROUP * D, (g + 1) * GROUP * D)
                sp.dma_start(acc[:, g * GROUP:(g + 1) * GROUP, :].rearrange("p j d -> p (j d)"),
                             x[:, cols]).then_inc(x_landed[g], 16)
            for dst, src in ((wv_sb[:, :], wv), (w_out_sb[:, :], w_out), (b_out_sb[:, :], b_out.broadcast_to([P, D])),
                             (router_b_sb[:, :], router_b.broadcast_to([P, E])),
                             (temp_sb[:, :], temperature.broadcast_to([P, 1]))):
                sp.dma_start(dst, src).then_inc(weights_landed, 16)
            sp.wait_ge(zeros_set, 1)
            ZR = ST * SLOT_TILES // P
            for r in range(0, ZR, 2):
                rows = slots_x.rearrange("(p r) d -> p (r d)", p=P)
                sp.dma_start(rows[:, r * D:(r + 2) * D], zeros[:, :]).then_inc(zeros_landed, 16)

            def stage(f_half, par):
                f = 2 * f_half + par
                sp.wait_ge(z_ready, 4 * (f - 1))
                sp.wait_ge(v_ready, f - 1)
                cols = bass.ds(f * (2 * P), 2 * P)
                sp.dma_start(xT_stage[par][:, :], xnT[:, cols]).then_inc(xT_staged[par], 16)

            sp.wait_ge(xnT_copied, NG)
            with sp.Fori(LOOP_FROM // 2, EARLY // 2) as i:
                stage(i, 1)
                stage(i + 1, 0)

            expert_reg = sp.alloc_register("expert_reg")
            ys = slots_y.rearrange("(k t p) d -> k p t d", t=2, p=P)
            xs = slots_x.rearrange("(k t p) d -> k p t d", t=2, p=P)

            def load_rows(k, q, r):
                if late(k, 2):
                    sp.wait_ge(xT_ready, k - 1)
                sp.dma_start(x_tile[r % 2][:, :, :],
                             xs[bass.ds(k, 1), :, :, :].rearrange("a p t d -> (a p) t d"))\
                    .then_inc(rows_landed[r % 2], 16)

            def load_weights(k, q, r):
                sp.reg_load(expert_reg, expert_i[0:1, bass.ds(k, 1)])
                e = bass.ds(sp.snap(expert_reg, min_val=0, max_val=E - 1), 1)
                if late(k, LOOP):
                    sp.wait_ge(y_ready, k - LOOP + 1)
                sp.dma_start(w_tile[r][:, :], w_expert[e, :, :].rearrange("a p n -> (a p) n"))\
                    .then_inc(w_landed[r], 16)

            def store_tile(k, q, r):
                sp.wait_ge(y_copied, k + 1)
                sp.dma_start(ys[bass.ds(k, 1), :, :, :].rearrange("a p t d -> (a p) t d"),
                             y_tile[r % 2][:, :, :]).then_inc(y_stored[r % 2], 16)

            def expert_step(q, r):
                weights, rows = ahead(LOOP - 1, q, r), ahead(4, q, r)
                if exists(weights[0]) and late(weights[0], LOOP):
                    load_weights(*weights)
                if exists(rows[0]):
                    load_rows(*rows)
                store_tile(*ahead(0, q, r))

            sp.wait_ge(experts_ready, 1)
            for k in range(LOOP):
                load_weights(*ahead(k, 0, 0))
            sp.wait_ge(scattered, 16 * NT * TOPK)
            for k in range(4):
                load_rows(*ahead(k, 0, 0))
            experts(sp, expert_step)

            for g in range(NG):
                sp.wait_ge(row_added[TOPK - 1], GROUP * (g + 1))
                sp.wait_ge(acc_added, GROUP // 2 * (g + 1))
                cols = slice(g * GROUP * D, (g + 1) * GROUP * D)
                sp.dma_start(out[:, cols], acc[:, g * GROUP:(g + 1) * GROUP, :].rearrange("p j d -> p (j d)"))\
                    .then_inc(out_stored, 16)
            sp.wait_ge(out_stored, 16 * NG)

        @block.gpsimd
        def _(pool):
            pool.memset(zeros[:, :], 0.0).then_inc(zeros_set, 1)
            pool.memset(ident[:, :], 0.0).then_inc(zeros_set, 1)
            pool.memset(eps_tile[:, :], LN_EPS).then_inc(consts_set, 1)
            pool.memset(ones[:, :], 1.0).then_inc(consts_set, 1)
            pool.memset(head_of_row[:, :], 1.0).then_inc(zeros_set, 1)
            pool.memset(earlier[:, :], 1.0).then_inc(zeros_set, 1)
            pool.memset(scan_keep[:, :, :], 1.0).then_inc(zeros_set, 1)
            for i in range(2):
                pool.memset(v_aug[i][:, :, :, VC:AUG], 1.0).then_inc(consts_set, 1)
            pool.wait_ge(zeros_set, 5)
            pool.affine_select(out=ident[:, :], in_=ident[:, :], compare_op=ALU.not_equal, fill=1.0, base=0,
                               pattern=[[-1, P]], channel_multiplier=1).then_inc(ident_set, 1)
            pool.affine_select(out=head_of_row[:, :], in_=head_of_row[:, :], compare_op=ALU.is_ge, fill=0.0, base=0,
                               pattern=[[-HD, HEADS]], channel_multiplier=1).then_inc(zeros_set, 1)
            pool.affine_select(out=earlier[:, :], in_=earlier[:, :], compare_op=ALU.is_ge, fill=0.0, base=-1,
                               pattern=[[1, P]], channel_multiplier=-1).then_inc(consts_set, 1)
            pool.wait_ge(zeros_set, 6)
            pool.affine_select(out=head_of_row[:, :], in_=head_of_row[:, :], compare_op=ALU.is_ge, fill=0.0,
                               base=HD - 1, pattern=[[HD, HEADS]], channel_multiplier=-1).then_inc(ident_set, 1)
            pool.memset(scan_keep[:, :, 0:1], 0.0).then_inc(consts_set, 1)
            pool.iota(rank_of_expert[:, :], pattern=[[-1, E]], base=E, channel_multiplier=0,
                      allow_small_or_imprecise_dtypes=True).then_inc(consts_set, 1)
            pool.iota(tile_number[:, :, :], pattern=[[1, SLOT_TILES], [0, E]], base=0, channel_multiplier=0,
                      allow_small_or_imprecise_dtypes=True).then_inc(consts_set, 1)

            pool.wait_ge(weights_landed, 16 * N_WEIGHTS)
            for g in range(NG):
                tiles = acc[:, g * GROUP:(g + 1) * GROUP, :]
                pool.wait_ge(xn_by_dve, g + 1)
                pool.wait_ge(xn_by_act, g + 1)
                pool.tensor_tensor(tiles, tiles, xn[:, g * GROUP:(g + 1) * GROUP, :], ALU.add)\
                    .then_inc(base_added, 1)
                pool.wait_ge(base_added, 2 * g + 1)
                pool.tensor_tensor(tiles, tiles, over_tiles(b_out_sb, GROUP), ALU.add).then_inc(base_added, 1)

            pool.wait_ge(zeros_landed, 16 * (ST * SLOT_TILES // P // 2))
            for k in range(TOPK):
                pool.wait_ge(slots_ready, k + 1)
                for j in range(NT):
                    i = routing_tile(j)
                    pool.indirect_dma_start(slots_x, bass.IndirectOffsetOnAxis(slot_i[k][:, i:i + 1], 0),
                                            xn[:, j, :], None).then_inc(scattered, 16)

            def weights_low(k, q, r):
                pool.wait_ge(w_high_ready, k + 1)
                pool.tensor_tensor(w_low[r % 2][:, :], w_tile[r][:, 0:2 * FF], w_high[r % 2][:, :].bitcast(F32),
                                   ALU.subtract).then_inc(w_low_ready, 1)

            experts(pool, lambda q, r: weights_low(*ahead(0, q, r)))

            pool.wait_ge(y_stored[0], 16 * ((SLOT_TILES + 1) // 2))
            pool.wait_ge(y_stored[1], 16 * (SLOT_TILES // 2))
            for j in range(NT):
                i = routing_tile(j)
                if j >= RING:
                    pool.wait_ge(row_added[1], j - RING + 1)
                for k in range(TOPK):
                    pool.indirect_dma_start(y_back[:, j % RING, k, :], None, slots_y,
                                            bass.IndirectOffsetOnAxis(slot_i[k][:, i:i + 1], 0))\
                        .then_inc(gathered[j % RING], 16)
            for r in range(RING):
                pool.wait_ge(gathered[r], 16 * TOPK * (NT // RING))

        CONSTS = 8

        @block.tensor
        def _(pe):
            def feature_weights():
                pe.wait_ge(diag_ready, 1)
                diag = proj_diag[:, :, :].rearrange("p h f -> p (h f)")
                pe.matmul(bank[2][:, :], wkT_sb[:, :], diag, start=True, stop=True).then_inc(w_feat_ready, 1)
                pe.matmul(bank[3][:, :], wqT_sb[:, :], diag, start=True, stop=True).then_inc(w_feat_ready, 1)

            def keep_warm(n, free_bank):
                for _ in range(n):
                    pe.matmul(bank[free_bank][:, 0:P], ones[:, :], ones[:, :], start=True, stop=True)

            def transposes(g):
                if g >= 2:
                    pe.wait_ge(xnT_copied, g - 1)
                pe.wait_ge(xn_by_dve, g + 1)
                pe.wait_ge(xn_by_act, g + 1)
                for t in range(GROUP):
                    mm = pe.transpose(bank[g % 2][:, t * P:(t + 1) * P], xn[:, g * GROUP + t, :], ident[:, :])
                mm.then_inc(xnT_ready, 1)

            def router(g):
                pe.wait_ge(xnT_copied, g + 1)
                for t in range(GROUP):
                    j = g * GROUP + t
                    i = routing_tile(j)
                    mm = pe.matmul(bank[ROUTE_BANK][:, i * E:(i + 1) * E], xnT[:, j * P:(j + 1) * P],
                                   router_sb[:, :], start=True, stop=True)
                mm.then_inc(scores_ready, 1)

            pe.wait_ge(consts_set, CONSTS)
            keep_warm(24, 4)
            pe.wait_ge(ident_set, 1)
            pe.wait_ge(feature_weights_landed, 16 * N_FEATURE_WEIGHTS)
            for g in range(NG):
                transposes(g)
                if g >= 1:
                    router(g - 1)
                    keep_warm(1, 4)
                if g == 1:
                    feature_weights()

            def xT(f, par, half):
                if isinstance(f, int):
                    return xnT[:, (2 * f + half) * P:(2 * f + half + 1) * P]
                return xT_stage[par][:, half * P:(half + 1) * P]

            def z(n, f, f_half, par):
                if n == 0 and not isinstance(f, int):
                    pe.wait_ge(xT_staged[par], 16 * (f_half + par - LOOP_FROM // 2))
                if late(f, 1):
                    pe.wait_ge(z_shifted, 4 * f + n - 3)
                pe.matmul(bank[Z_BANK + n][:, :], xT(f, par, n % 2), w_feat[:, n // 2, :],
                          start=True, stop=True).then_inc(z_ready, 1)

            def v(f, par):
                if late(f, 1):
                    pe.wait_ge(v_copied, f)
                for h in range(2):
                    mm = pe.matmul(bank[V_BANK][:, h * P:(h + 1) * P], xT(f, par, h),
                                   wv_sb[:, :], start=True, stop=True)
                mm.then_inc(v_ready, 1)

            def kv(b, par):
                pe.wait_ge(feat_ready, 4 * b + 2)
                pe.wait_ge(v_copied, b + 1)
                if late(b, 1):
                    pe.wait_ge(att_ready, b)
                if isinstance(b, int) and b == EARLY:
                    pe.wait_ge(y_copied, SLOT_TILES)
                for c in range(CH):
                    for h in range(2):
                        mm = pe.matmul(bank[KV_BANK][:, c * AUG:(c + 1) * AUG], feat[par][h][:, c * P:(c + 1) * P],
                                       v_aug[par][:, h, c, :], start=(h == 0), stop=(h == 1))
                mm.then_inc(kv_ready, 1)

            def qT(h, b, par, route):
                pe.wait_ge(feat_ready, 4 * b + 3 + h)
                if h == 1 and route:
                    pe.wait_ge(qT_copied, 2 * b + 1)
                elif h == 1:
                    pe.wait_ge(slots_ready, TOPK)
                    pe.wait_ge(qT_copied, 2 * b)
                elif late(b, 2):
                    pe.wait_ge(acc_added, b - 1)
                for c in range(CH):
                    mm = pe.transpose(bank[qT_bank(h, route)][:, c * P:(c + 1) * P],
                                      feat[par][2 + h][:, c * P:(c + 1) * P], ident[:, :])
                mm.then_inc(qT_ready, 1)

            def numden(b, par):
                pe.wait_ge(qT_copied, 2 * b + 2)
                pe.wait_ge(kv_masked, b + 1)
                for h in range(2):
                    for c in range(CH):
                        at = ND + (h * CH + c) * AUG
                        mm = pe.matmul(bank[KV_BANK][:, at:at + AUG], qT_sb[h][:, c * P:(c + 1) * P],
                                       kv_sb[par][:, c, :], start=True, stop=True)
                mm.then_inc(nd_ready, 1)

            def attention_T(b):
                pe.wait_ge(att_ready, b + 1)
                for h in range(2):
                    mm = pe.transpose(bank[V_BANK][:, (2 + h) * P:(3 + h) * P], att[:, h * P:(h + 1) * P],
                                      ident[:, :])
                mm.then_inc(attT_ready, 1)

            def project(b, last, route):
                pe.wait_ge(attT_copied, b + 1)
                if not last:
                    pe.wait_ge(qT_copied, 2 * b + (4 if route else 3))
                for h in range(2):
                    mm = pe.matmul(bank[QT_BANK][:, h * P:(h + 1) * P], attT[:, h * P:(h + 1) * P],
                                   w_out_sb[:, :], start=True, stop=True)
                mm.then_inc(proj_ready, 1)

            def route_link(n):
                part = n % 5
                if n < 0:
                    router(NG - 1)
                elif n >= 5 * SINKHORN_ITERS:
                    if n == 5 * SINKHORN_ITERS + 1:
                        pe.wait_ge(mask_ready, 1)
                        pe.matmul(bank[ROUTE_BANK][:, 0:W], earlier[:, :], mask[:, :], start=True, stop=True)
                        pe.matmul(bank[ROUTE_BANK][:, W:2 * W], ones[:, :], mask[:, :], start=True, stop=True)\
                            .then_inc(counts_ready, 1)
                elif part == 2:
                    pe.wait_ge(row_normed, n // 5 + 1)
                    for h in range(2):
                        mm = pe.transpose(bank[ROUTE_BANK][:, h * P:(h + 1) * P], row_log[:, h * P:(h + 1) * P],
                                          ident[:, :])
                    mm.then_inc(cols_in, 1)
                elif part == 4:
                    pe.wait_ge(col_normed, n // 5 + 1)
                    for h in range(2):
                        mm = pe.transpose(bank[ROUTE_BANK][:, W + h * P:W + (h + 1) * P],
                                          col_log[:, h * P:(h + 1) * P], ident[:, :])
                    mm.then_inc(rows_in, 1)

            def step(b, b_half, par, front=True, back=True, tail=True, route=False):
                f, f_half, f_par = b + 1, b_half + par, 1 - par
                link = LINKS * f if route else None
                if front:
                    z(0, f, f_half, f_par)
                elif back:
                    keep_warm(6, ROUTE_BANK)
                if route:
                    route_link(link - 1)
                if front:
                    z(1, f, f_half, f_par)
                if route:
                    for n in range(3):
                        route_link(link + n)
                    z(2, f, f_half, f_par)
                    route_link(link + 3)
                    route_link(link + 4)
                    z(3, f, f_half, f_par)
                    route_link(link + 5)
                    route_link(link + 6)
                if front:
                    v(f, f_par)
                if back:
                    kv(b, par)
                if tail:
                    attention_T(b - 1)
                if not front and back:
                    keep_warm(3, ROUTE_BANK)
                if back:
                    qT(0, b, par, route)
                if front and not route:
                    z(2, f, f_half, f_par)
                if back:
                    qT(1, b, par, route)
                if route and back:
                    route_link(link + LINKS)
                if front and not route:
                    z(3, f, f_half, f_par)
                if tail:
                    project(b - 1, last=not back, route=route)
                if not front and back:
                    keep_warm(3, Z_BANK)
                if back:
                    numden(b, par)

            pe.wait_ge(xnT_copied, NG)
            pe.wait_ge(w_feat_copied, 2)
            attend_early(pe, step)

            def rows_T(k, q, r):
                pe.wait_ge(rows_landed[r % 2], 16 * (before(q, r) + 1))
                if late(k, 2):
                    pe.wait_ge(xT_low_ready, k - 1)
                for t in range(2):
                    mm = pe.transpose(bank[r % 2][:, t * P:(t + 1) * P], x_tile[r % 2][:, t, :], ident[:, :])
                mm.then_inc(xT_ready, 1)

            def up(k, q, r):
                par = r % 2
                pe.wait_ge(xT_low_ready, k + 1)
                pe.wait_ge(w_low_ready, k + 1)
                if late(k, 2):
                    pe.wait_ge(hidden_ready, k - 1)
                for half in range(2):
                    for c in range(FC):
                        cols = slice(half * FF + c * P, half * FF + (c + 1) * P)
                        to = bank[2 + 2 * half + par][:, c * ST:(c + 1) * ST]
                        pe.matmul(to, w_high[par][:, cols], xT_high[par][:, :], start=True, stop=False)
                        pe.matmul(to, w_high[par][:, cols], xT_low[par][:, :], start=False, stop=False)
                        mm = pe.matmul(to, w_low[par][:, cols], xT_high[par][:, :], start=False, stop=True)
                    mm.then_inc(up_ready, 1)

            def down(k, q, r):
                pe.wait_ge(hidden_ready, k + 1)
                if late(k, 2):
                    pe.wait_ge(y_copied, k - 1)
                for t in range(2):
                    for c in range(FC):
                        at = 2 * FF + c * D
                        mm = pe.matmul(bank[6 + r % 2][:, t * D:(t + 1) * D], hidden[r % 2][:, c, t * P:(t + 1) * P],
                                       w_tile[r][:, at:at + D], start=(c == 0), stop=(c == FC - 1))
                mm.then_inc(y_ready, 1)

            def expert_step(q, r):
                if exists(ahead(2, q, r)[0]):
                    rows_T(*ahead(2, q, r))
                if exists(ahead(1, q, r)[0]):
                    up(*ahead(1, q, r))
                down(*ahead(0, q, r))

            pe.wait_ge(v_copied, EARLY + 1)
            pe.wait_ge(z_shifted, 4 * (EARLY + 1))
            pe.wait_ge(acc_added, EARLY - 1)
            pe.wait_ge(att_ready, EARLY)
            rows_T(0, 0, 0)
            rows_T(1, 0, 1)
            up(0, 0, 0)
            experts(pe, expert_step)
            attend_late(step)

        @block.scalar
        def _(act):
            act.preload_act_table_set(SQRT_TABLE)
            for dst, src in ((router_sb[:, :], router_wT), (proj_sb[:, :], proj), (wkT_sb[:, :], wkT),
                             (wqT_sb[:, :], wqT)):
                act.dma_start(dst, src).then_inc(feature_weights_landed, 16)

            act.wait_ge(consts_set, CONSTS)

            def root(g):
                act.wait_ge(moments_done, g + 1)
                tiles = slice(g * GROUP, (g + 1) * GROUP)
                act.activation(std[:, tiles], moments[:, tiles, 1], ACT.Sqrt, bias=eps_tile[:, :])\
                    .then_inc(std_done, 1)

            def normalise(g):
                act.wait_ge(shift_done, g + 1)
                for j in range((g + 1) * GROUP - BY_ACT, (g + 1) * GROUP):
                    ins = act.activation(xn[:, j, :], acc[:, j, :], ACT.Identity, bias=shift[:, j:j + 1],
                                         scale=rstd[:, j:j + 1])
                ins.then_inc(xn_by_act, 1)

            def copy_xnT(g):
                act.wait_ge(xnT_ready, g + 1)
                act.copy(xnT[:, g * GROUP * P:(g + 1) * GROUP * P], bank[g % 2][:, :]).then_inc(xnT_copied, 1)

            for g in range(NG + 2):
                if g < NG:
                    root(g)
                if 1 <= g <= NG:
                    normalise(g - 1)
                if g >= 2:
                    copy_xnT(g - 2)
                if g == 3:
                    for n in range(2):
                        act.wait_ge(w_feat_ready, n + 1)
                        act.copy(w_feat[:, n, :], bank[2 + n][:, :]).then_inc(w_feat_copied, 1)
            act.preload_act_table_set(EXP_LN_TABLE)

            def features(n, f, par):
                act.wait_ge(z_shifted, 4 * f + n + 1)
                if late(f, 2):
                    if n < 2:
                        act.wait_ge(kv_ready, f - 1)
                    else:
                        act.wait_ge(qT_ready, 2 * f - 4 + n - 1)
                act.activation(feat[par][n][:, :], z_sb[n][:, :], ACT.Exp).then_inc(feat_ready, 1)

            def copy_v(f, par):
                act.wait_ge(v_ready, f + 1)
                if late(f, 2):
                    act.wait_ge(kv_ready, f - 1)
                act.copy(v_aug[par][:, :, :, 0:VC], bank[V_BANK][:, 0:2 * P]
                         .rearrange("p (h c v) -> p h c v", h=2, c=CH)).then_inc(v_copied, 1)

            def copy_qT(h, b, route):
                act.wait_ge(qT_ready, 2 * b + h + 1)
                if late(b, 1):
                    act.wait_ge(nd_ready, b)
                act.copy(qT_sb[h][:, :], bank[qT_bank(h, route)][:, :]).then_inc(qT_copied, 1)

            def copy_attT(b):
                act.wait_ge(attT_ready, b + 1)
                if late(b, 1):
                    act.wait_ge(proj_ready, b)
                act.copy(attT[:, :], bank[V_BANK][:, 2 * P:4 * P]).then_inc(attT_copied, 1)

            def route_link(n):
                it, part = n // 5, n % 5
                if n == 5 * SINKHORN_ITERS:
                    act.wait_ge(rows_in, SINKHORN_ITERS)
                    act.activation(gate_exp[:, :], bank[ROUTE_BANK][:, W:2 * W], ACT.Exp).then_inc(gates_exped, 1)
                elif n < 5 * SINKHORN_ITERS:
                    if part == 0:
                        act.wait_ge(row_shifted, it + 1)
                        act.activation(row_exp[:, :], row_shift[:, :], ACT.Exp).then_inc(row_exped, 1)
                    elif part == 1:
                        act.wait_ge(row_summed, it + 1)
                        act.activation(row_ln[:, :], row_sum[:, :], ACT.Ln).then_inc(row_lned, 1)
                    elif part == 3:
                        act.wait_ge(col_maxed, it + 1)
                        act.activation(col_exp[:, :], bank[ROUTE_BANK][:, 0:W], ACT.Exp, bias=col_negmax[:, :],
                                       accum_out=col_sum[:, :]).then_inc(col_summed, 1)
                        act.wait_ge(col_summed, it + 1)
                        act.activation(col_ln[:, :], col_sum[:, :], ACT.Ln).then_inc(col_lned, 1)

            def step(b, b_half, par, front=True, back=True, tail=True, route=False):
                f, f_par = b + 1, 1 - par
                link = LINKS * f if route else None
                def links(*slots):
                    for n in slots:
                        if route:
                            route_link(link + n)

                links(0)
                if front:
                    features(0, f, f_par)
                links(1, 2)
                if front:
                    features(1, f, f_par)
                links(3, 4)
                if route:
                    features(2, f, f_par)
                    links(5, 6, 7)
                if back:
                    copy_qT(0, b, route)
                if tail:
                    copy_attT(b - 1)
                if route:
                    copy_v(f, f_par)
                if back:
                    copy_qT(1, b, route)
                if front and not route:
                    copy_v(f, f_par)
                    features(2, f, f_par)
                if front:
                    features(3, f, f_par)

            attend_early(act, step)

            def rows_high(k, q, r):
                act.wait_ge(xT_ready, k + 1)
                if late(k, 2):
                    act.wait_ge(up_ready, 2 * k - 2)
                act.copy(xT_high[r % 2][:, :], bank[r % 2][:, 0:ST]).then_inc(xT_high_ready, 1)

            def weights_high(k, q, r):
                act.wait_ge(w_landed[r], 16 * (q + 1))
                act.copy(w_high[r % 2][:, :], w_tile[r][:, 0:2 * FF]).then_inc(w_high_ready, 1)

            def relu(k, q, r):
                act.wait_ge(up_ready, 2 * k + 1)
                if late(k, 2):
                    act.wait_ge(hidden_ready, k - 1)
                act.activation(gate_act[r % 2][:, :], bank[2 + r % 2][:, :], ACT.Relu).then_inc(relu_done, 1)

            def expert_step(q, r):
                if exists(ahead(2, q, r)[0]):
                    rows_high(*ahead(2, q, r))
                    weights_high(*ahead(2, q, r))
                if exists(ahead(1, q, r)[0]):
                    relu(*ahead(1, q, r))

            for k in range(2):
                weights_high(k, 0, k)
            for k in range(2):
                rows_high(k, 0, k)
            relu(0, 0, 0)
            experts(act, expert_step)
            attend_late(step)

        @block.vector
        def _(dve):
            dve.memset(chunk_mask[:, :], 0.0).then_inc(chunk_mask_set, 1)
            dve.wait_ge(chunk_mask_set, 1)
            for m in range(HC):
                rows = slice(F * m, F * (m + 1))
                dve.memset(chunk_mask[rows, HD * m:HD * (m + 1)], 1.0).then_inc(chunk_mask_set, 1)
                dve.memset(chunk_mask[rows, VC + m:VC + m + 1], 1.0).then_inc(chunk_mask_set, 1)

            def statistics(g):
                dve.wait_ge(x_landed[g], 16)
                for t in range(GROUP):
                    ins = dve.bn_stats(stats[:, g * GROUP + t, :], acc[:, g * GROUP + t, :])
                ins.then_inc(stats_done, 1)
                dve.wait_ge(stats_done, g + 1)
                for t in range(GROUP):
                    ins = dve.bn_aggr(moments[:, g * GROUP + t, :], stats[:, g * GROUP + t, :])
                ins.then_inc(moments_done, 1)

            def normalise(g):
                tiles = slice(g * GROUP, (g + 1) * GROUP)
                dve.wait_ge(std_done, g + 1)
                dve.reciprocal(rstd[:, tiles], std[:, tiles]).then_inc(rstd_done, 1)
                dve.wait_ge(rstd_done, g + 1)
                dve.scalar_tensor_tensor(shift[:, tiles], moments[:, tiles, 0], -1.0, rstd[:, tiles],
                                         ALU.mult, ALU.mult).then_inc(shift_done, 1)
                for t in range(GROUP - BY_ACT):
                    j = g * GROUP + t
                    ins = dve.tensor_scalar(xn[:, j, :], acc[:, j, :], moments[:, j, 0:1], rstd[:, j:j + 1],
                                            ALU.subtract, ALU.mult)
                ins.then_inc(xn_by_dve, 1)

            for g in range(NG + 1):
                if g < NG:
                    statistics(g)
                if g >= 1:
                    normalise(g - 1)
                if g == 1:
                    dve.wait_ge(feature_weights_landed, 16 * N_FEATURE_WEIGHTS)
                    dve.wait_ge(ident_set, 2)
                    dve.tensor_tensor(proj_diag[:, :, :], over_tiles(proj_sb, HEADS), wide(head_of_row, F), ALU.mult)\
                        .then_inc(diag_ready, 1)

            def args(n):
                return bank[Z_BANK + n][:, :].rearrange("p (h f) -> p h f", f=F)

            def z_max(n, f):
                dve.wait_ge(z_ready, 4 * f + n + 1)
                dve.tensor_reduce(neg_max[n][:, :], args(n), AX_X, ALU.max, negate=True).then_inc(z_negmax, 1)

            def z_shift(n, f):
                dve.wait_ge(z_negmax, 4 * f + n + 1)
                if late(f, 1):
                    dve.wait_ge(feat_ready, 4 * f + n - 3)
                dve.tensor_tensor(z_sb[n][:, :].rearrange("p (h f) -> p h f", f=F), args(n), wide(neg_max[n], F),
                                  ALU.add).then_inc(z_shifted, 1)

            def mask_kv(b, par):
                dve.wait_ge(kv_ready, b + 1)
                if late(b, 2):
                    dve.wait_ge(nd_ready, b - 1)
                dve.tensor_tensor(kv_sb[par][:, :, :], bank[KV_BANK][:, 0:CH * AUG].rearrange("p (c a) -> p c a", c=CH),
                                  over_tiles(chunk_mask, CH), ALU.mult).then_inc(kv_masked, 1)

            nd = bank[KV_BANK][:, ND:ND + 2 * CH * AUG].rearrange("p (c a) -> p c a", a=AUG)

            def denominators(b):
                dve.wait_ge(nd_ready, b + 1)
                dve.tensor_scalar(den[:, :, :], nd[:, :, VC:AUG], DEN_EPS, None, ALU.add).then_inc(den_step, 1)

            def invert(b):
                dve.wait_ge(den_step, 2 * b + 1)
                dve.reciprocal(inv_den[:, :, :], den[:, :, :]).then_inc(den_step, 1)

            def divide(b):
                dve.wait_ge(den_step, 2 * b + 2)
                if late(b, 1):
                    dve.wait_ge(attT_ready, b)
                dve.tensor_tensor(att[:, :].rearrange("p (c m d) -> p c m d", c=2 * CH, m=HC),
                                  nd[:, :, 0:VC].rearrange("p c (m d) -> p c m d", m=HC),
                                  inv_den[:, :, :].unsqueeze(3).broadcast_to([P, 2 * CH, HC, HD]), ALU.mult)\
                    .then_inc(att_ready, 1)

            def add_projection(b):
                dve.wait_ge(proj_ready, b + 1)
                if not late(b, 1):
                    dve.wait_ge(base_added, 2 * NG)
                tiles = acc[:, bass.ds(2 * b, 2), :]
                dve.tensor_tensor(tiles, bank[QT_BANK][:, 0:2 * P].rearrange("p (t d) -> p t d", t=2), tiles, ALU.add)\
                    .then_inc(acc_added, 1)

            def combine(g, k):
                if k == 0:
                    dve.wait_ge(acc_added, min((g + 1) * GROUP // 2, EARLY + g))
                for j in range(g * GROUP, (g + 1) * GROUP):
                    if k == 0:
                        dve.wait_ge(gathered[j % RING], 16 * TOPK * (j // RING + 1))
                    else:
                        dve.wait_ge(row_added[0], j + 1)
                    i = routing_tile(j)
                    dve.scalar_tensor_tensor(acc[:, j, :], y_back[:, j % RING, k, :], weight[k][:, i:i + 1],
                                             acc[:, j, :], ALU.mult, ALU.add).then_inc(row_added[k], 1)

            own = [0]

            def settle(ins):
                own[0] += 1
                ins.then_inc(route_step, 1)
                dve.wait_ge(route_step, own[0])

            def choose(k, values):
                settle(dve.tensor_reduce(top[k][:, :], by_tile(values), AX_X, ALU.max))
                settle(dve.tensor_tensor(by_tile(is_best), by_tile(values), wide(top[k], E), ALU.is_equal))
                settle(dve.tensor_tensor(by_tile(ranked), by_tile(is_best), over_tiles(rank_of_expert, NT), ALU.mult))
                settle(dve.tensor_reduce(best_rank[:, :], by_tile(ranked), AX_X, ALU.max))
                settle(dve.tensor_tensor(by_tile(chosen[k]), by_tile(ranked), wide(best_rank, E), ALU.is_equal))

            def route_link(n):
                it, part = n // 5, n % 5
                if n < 5 * SINKHORN_ITERS:
                    if part == 0:
                        if it == 0:
                            dve.wait_ge(scores_ready, NG)
                            settle(dve.tensor_tensor(
                                by_tile(scores), bank[ROUTE_BANK][:, 0:W].rearrange("p (i e) -> p i e", e=E),
                                over_tiles(router_b_sb, NT), ALU.add))
                            settle(dve.tensor_scalar(scores[:, :], scores[:, :], inv_temp[:, :], None, ALU.mult))
                            src = scores[:, :]
                        else:
                            dve.wait_ge(rows_in, it)
                            src = bank[ROUTE_BANK][:, W:2 * W]
                        src = src.rearrange("p (i e) -> p i e", e=E)
                        settle(dve.tensor_reduce(row_max[:, :], src, AX_X, ALU.max))
                        dve.tensor_tensor(by_tile(row_shift), src, wide(row_max, E), ALU.subtract)\
                            .then_inc(row_shifted, 1)
                    elif part == 1:
                        dve.wait_ge(row_exped, it + 1)
                        dve.tensor_reduce(row_sum[:, :], by_tile(row_exp), AX_X, ALU.add).then_inc(row_summed, 1)
                    elif part == 2:
                        dve.wait_ge(row_lned, it + 1)
                        dve.tensor_tensor(by_tile(row_log), by_tile(row_shift), wide(row_ln, E), ALU.subtract)\
                            .then_inc(row_normed, 1)
                    elif part == 3:
                        dve.wait_ge(cols_in, it + 1)
                        dve.tensor_reduce(col_negmax[:, :], bank[ROUTE_BANK][:, 0:W], AX_X, ALU.max, negate=True)\
                            .then_inc(col_maxed, 1)
                    elif part == 4:
                        dve.wait_ge(col_lned, it + 1)
                        dve.tensor_scalar(col_log[:, :], bank[ROUTE_BANK][:, 0:W], col_negmax[:, :], col_ln[:, :],
                                          ALU.add, ALU.subtract).then_inc(col_normed, 1)
                elif n == 5 * SINKHORN_ITERS:
                    dve.wait_ge(gates_exped, 1)
                    settle(dve.tensor_reduce(gate_sum[:, :], by_tile(gate_exp), AX_X, ALU.add))
                    settle(dve.tensor_scalar(gate_sum[:, :], gate_sum[:, :], GATE_EPS, None, ALU.add))
                    settle(dve.reciprocal(gate_inv[:, :], gate_sum[:, :]))
                    settle(dve.tensor_tensor(by_tile(gates), by_tile(gate_exp), wide(gate_inv, E), ALU.mult))
                    choose(0, gates)
                elif n == 5 * SINKHORN_ITERS + 1:
                    settle(dve.scalar_tensor_tensor(rest[:, :], chosen[0][:, :], -4.0, gates[:, :], ALU.mult, ALU.add))
                    choose(1, rest)
                    dve.tensor_tensor(mask[:, :], chosen[0][:, :], chosen[1][:, :], ALU.add).then_inc(mask_ready, 1)
                elif n == 5 * SINKHORN_ITERS + 2:
                    place()
                elif n == 5 * SINKHORN_ITERS + 3:
                    settle(dve.tensor_tensor(top_sum[:, :], top[0][:, :], top[1][:, :], ALU.add))
                    settle(dve.tensor_scalar(top_sum[:, :], top_sum[:, :], GATE_EPS, None, ALU.add))
                    settle(dve.reciprocal(top_inv[:, :], top_sum[:, :]))
                    for k in range(TOPK):
                        settle(dve.tensor_tensor(weight[k][:, :], top[k][:, :], top_inv[:, :], ALU.mult))

            def place():
                dve.wait_ge(counts_ready, 1)
                settle(dve.tensor_copy(totals[:, :, :].rearrange("p e i -> p i e"),
                                       bank[ROUTE_BANK][:, W:2 * W].rearrange("p (i e) -> p i e", e=E)))
                settle(dve.tensor_tensor_scan(prefix[:, :, :].rearrange("p e i -> p (e i)"),
                                              scan_keep[:, :, :].rearrange("p e i -> p (e i)"),
                                              totals[:, :, :].rearrange("p e i -> p (e i)"), 0.0, ALU.mult, ALU.add))
                settle(dve.tensor_scalar(padded_i[:, :], prefix[:, :, NT - 1], float(ST - 1), None, ALU.add))
                settle(dve.tensor_scalar(tiles_i[:, :], padded_i[:, :], ST.bit_length() - 1, None,
                                         ALU.logical_shift_right))
                settle(dve.tensor_copy(tiles_f[:, :], tiles_i[:, :]))
                settle(dve.tensor_tensor_scan(tiles_end[:, :], ones[:, 0:E], tiles_f[:, :], 0.0, ALU.mult, ALU.add))
                settle(dve.tensor_tensor(first_slot[:, :], tiles_end[:, :], tiles_f[:, :], ALU.subtract))
                settle(dve.tensor_scalar(first_slot[:, :], first_slot[:, :], float(ST), None, ALU.mult))
                settle(dve.tensor_tensor(start[:, :, :], prefix[:, :, :], totals[:, :, :], ALU.subtract))
                settle(dve.tensor_tensor(start[:, :, :], start[:, :, :], wide(first_slot, NT), ALU.add))
                settle(dve.tensor_tensor(by_tile(position), bank[ROUTE_BANK][:, 0:W].rearrange("p (i e) -> p i e", e=E),
                                         start[:, :, :].rearrange("p e i -> p i e"), ALU.add))
                for k in range(TOPK):
                    settle(dve.tensor_tensor(picked[k][:, :], chosen[k][:, :], position[:, :], ALU.mult))
                    settle(dve.tensor_reduce(slot_f[k][:, :], by_tile(picked[k]), AX_X, ALU.add))
                    dve.tensor_copy(slot_i[k][:, :], slot_f[k][:, :]).then_inc(slots_ready, 1)
                settle(dve.tensor_tensor(past[:, :, :], tile_number[:, :, :], over_tiles(tiles_end, SLOT_TILES), ALU.is_ge))
                settle(dve.tensor_reduce(expert_f[:, :], past[:, :, :], AX_X, ALU.add))
                dve.tensor_scalar(expert_i[:, :], expert_f[:, :], float(E - 1), None, ALU.min).then_inc(experts_ready, 1)

            def step(b, b_half, par, front=True, back=True, tail=True, route=False, group=None):
                f = b + 1
                link = LINKS * f if route else None
                divides = tail and not (isinstance(b, int) and b == EARLY)
                if divides:
                    denominators(b - 1)
                    invert(b - 1)
                    divide(b - 1)
                if front:
                    z_max(0, f)
                if route:
                    route_link(link)
                if front and not route:
                    z_max(1, f)
                if front:
                    z_shift(0, f)
                if route:
                    route_link(link + 1)
                    z_max(1, f)
                    route_link(link + 2)
                if front:
                    z_shift(1, f)
                if route:
                    route_link(link + 3)
                if back and not route:
                    mask_kv(b, par)
                if group is not None:
                    combine(group, 0)
                if front:
                    z_max(2, f)
                if group is not None:
                    combine(group, 1)
                if route:
                    route_link(link + 4)
                if front:
                    z_shift(2, f)
                if route:
                    route_link(link + 5)
                if front:
                    z_max(3, f)
                if route:
                    route_link(link + 6)
                    z_shift(3, f)
                    route_link(link + 7)
                if back and route:
                    mask_kv(b, par)
                    for n in range(LAST_LINKS):
                        route_link(link + LINKS + n)
                if tail:
                    if group is not None:
                        dve.wait_ge(row_added[TOPK - 1], (group + 1) * GROUP)
                    add_projection(b - 1)
                if front and not route:
                    z_shift(3, f)

            dve.wait_ge(chunk_mask_set, 1 + 2 * HC)
            dve.wait_ge(consts_set, CONSTS)
            dve.wait_ge(weights_landed, 16 * N_WEIGHTS)
            settle(dve.tensor_scalar(temp_lim[:, :], temp_sb[:, :], 0.1, None, ALU.max))
            settle(dve.reciprocal(inv_temp[:, :], temp_lim[:, :]))
            attend_early(dve, step)
            denominators(EARLY - 1)
            invert(EARLY - 1)
            divide(EARLY - 1)

            def rows_low(k, q, r):
                dve.wait_ge(xT_high_ready, k + 1)
                dve.tensor_tensor(xT_low[r % 2][:, :], bank[r % 2][:, 0:ST], xT_high[r % 2][:, :].bitcast(F32),
                                  ALU.subtract).then_inc(xT_low_ready, 1)

            def multiply(k, q, r):
                dve.wait_ge(relu_done, k + 1)
                dve.wait_ge(up_ready, 2 * k + 2)
                if late(k, 2):
                    dve.wait_ge(y_ready, k - 1)
                dve.tensor_tensor(hidden[r % 2][:, :, :].rearrange("p c s -> p (c s)"), bank[4 + r % 2][:, :],
                                  gate_act[r % 2][:, :], ALU.mult).then_inc(hidden_ready, 1)

            def copy_y(k, q, r):
                dve.wait_ge(y_ready, k + 1)
                if late(k, 2):
                    dve.wait_ge(y_stored[r % 2], 16 * before(q, r))
                dve.tensor_copy(y_tile[r % 2][:, :, :].rearrange("p t d -> p (t d)"), bank[6 + r % 2][:, 0:2 * D])\
                    .then_inc(y_copied, 1)

            def expert_step(q, r):
                if exists(ahead(2, q, r)[0]):
                    rows_low(*ahead(2, q, r))
                if exists(ahead(1, q, r)[0]):
                    multiply(*ahead(1, q, r))
                copy_y(*ahead(0, q, r))

            rows_low(0, 0, 0)
            rows_low(1, 0, 1)
            multiply(0, 0, 0)
            experts(dve, expert_step)

            def late_step(b, b_half, par, front, back):
                group = b - EARLY - 1 if EARLY < b <= EARLY + NG else None
                step(b, b_half, par, front=front, back=back, group=group)

            attend_late(late_step)
            for g in range(NB - EARLY, NG):
                combine(g, 0)
                combine(g, 1)


def kernel(L0_attn_x, L0_attn_w_qkv, L0_attn_w_out, L0_attn_b_out, L0_attn_proj, L0_ffn_router_w, L0_ffn_router_b,
           L0_ffn_temperature, L0_ffn_wg, L0_ffn_wp, L0_ffn_wo):
    import numpy as np
    import concourse.bacc as bacc
    from concourse.bass_utils import run_bass_kernel_spmd

    x = np.asarray(L0_attn_x)
    B, T, D = x.shape
    NT = B * T // P
    w_qkv = np.asarray(L0_attn_w_qkv)
    wg, wp, wo = (np.asarray(a) for a in (L0_ffn_wg, L0_ffn_wp, L0_ffn_wo))
    E, _, FF = wg.shape
    wo_rows = wo.reshape(E, FF // P, P, D).transpose(0, 2, 1, 3).reshape(E, P, FF // P * D)
    arrays = {
        "x_dram": x.reshape(NT, P, D).transpose(1, 0, 2).reshape(P, NT * D),
        "wqT_dram": w_qkv[:, 0:D].T,
        "wkT_dram": w_qkv[:, D:2 * D].T,
        "wv_dram": w_qkv[:, 2 * D:3 * D],
        "w_out_dram": np.asarray(L0_attn_w_out),
        "b_out_dram": np.asarray(L0_attn_b_out).reshape(1, D),
        "proj_dram": np.asarray(L0_attn_proj).reshape(D, -1),
        "router_wT_dram": np.asarray(L0_ffn_router_w).T,
        "router_b_dram": np.asarray(L0_ffn_router_b).reshape(1, E),
        "temperature_dram": np.asarray(L0_ffn_temperature).reshape(1, 1),
        "w_expert_dram": np.concatenate([wg, wp, wo_rows], axis=2),
    }
    arrays = {n: np.ascontiguousarray(a) for n, a in arrays.items()}
    nc = bacc.Bacc("TRN2", target_bir_lowering=False, num_devices=1)
    args = [nc.dram_tensor(n, a.shape, mybir.dt.from_np(a.dtype), kind="ExternalInput").ap() for n, a in arrays.items()]
    out = nc.dram_tensor("out_dram", (P, NT * D), F32, kind="ExternalOutput").ap()
    build_program(nc, *args, out)
    r = run_bass_kernel_spmd(nc, [arrays], core_ids=[0])
    got = np.asarray(r.results[0]["out_dram"])
    return got.reshape(P, NT, D).transpose(1, 0, 2).reshape(B, T, D)
```
